# Optimizing a Trainium2 kernel written in Bass

```python
import numpy as np
import jax
import jax.numpy as jnp

def _softmax(x, axis=-1):
    return jax.nn.softmax(x, axis=axis)

def _gelu(x):
    return jax.nn.gelu(x, approximate=True)

def _silu(x):
    return jax.nn.silu(x)

def _sigmoid(x):
    return jax.nn.sigmoid(x)

def _layernorm(x, axis=-1, eps=1e-05):
    m = jnp.mean(x, axis=axis, keepdims=True)
    v = jnp.var(x, axis=axis, keepdims=True)
    return (x - m) / jnp.sqrt(v + eps)

def _scatter_add(tgt, idx, src, axis=0):
    return tgt.at[idx].add(src)

def _segment_sum(src, seg, n):
    return jax.ops.segment_sum(src, seg, n)
kernel_name = 'mk_gnn_resnorm_d2_gnn_r32_6f61de'

def setup_inputs(seed: int=0):
    np.random.seed(seed)
    _w = jnp.asarray

    def _rec_inputs():
        import jax
        import jax.numpy as jnp
        _gk = jax.random.key(seed)
        x = -0.0004287 + 1 * jax.random.normal(jax.random.fold_in(_gk, 1), (25000, 160), jnp.float32)
        src = jax.random.randint(jax.random.fold_in(_gk, 2), (25000,), 0, 25000, jnp.int32)
        dst = jax.random.randint(jax.random.fold_in(_gk, 3), (25000,), 0, 25000, jnp.int32)
        _o = jnp.argsort(dst, stable=True)
        src = src[_o]
        dst = dst[_o]
        edge_attr_4 = 0.000452788 + 0.999756 * jax.random.normal(jax.random.fold_in(_gk, 12), (25000, 4), jnp.float32)
        edge_attr_64 = 0.000127647 + 1.00004 * jax.random.normal(jax.random.fold_in(_gk, 13), (25000, 64), jnp.float32)
        edge_attr_8 = jax.random.uniform(jax.random.fold_in(_gk, 14), (25000, 8), jnp.float32, 0.0, 1)
        node_vec1 = jax.random.uniform(jax.random.fold_in(_gk, 16), (25000, 1), jnp.float32, 0.0, 1)
        return (x, src, dst, edge_attr_4, edge_attr_64, edge_attr_8, node_vec1)
    x, src, dst, edge_attr_4, edge_attr_64, edge_attr_8, node_vec1 = _rec_inputs()

    def _L0_gnn_setup():
        import jax, jax.numpy as jnp
        import numpy as np
        N = 25000
        E = 12500
        MUL_S, MUL_V = (64, 32)
        NB, NH = (8, 64)
        WNUM = 64 + 64 + 32 + 32 + 32
        AVG_NEI = 16.0
        EPS = 1e-05
        INV_SQRT3 = 1.0 / np.sqrt(3.0)
        INV_SQRT2 = 1.0 / np.sqrt(2.0)

        def _split(x):
            return (x[:, :MUL_S], x[:, MUL_S:].reshape(-1, MUL_V, 3))

        def _forward(node_hiddens, edge_sh, edge_attr, W1_0, W1_1, Wfc1, Wfc2, Wfc3, W2_0, W2_1, Wsc0, Wsc1, g0, g1, edge_src, edge_dst):
            s_in, v_in = _split(node_hiddens)
            sc_s = s_in @ Wsc0 / np.sqrt(MUL_S)
            sc_v = jnp.einsum('nuc,uv->nvc', v_in, Wsc1) / np.sqrt(MUL_V)
            s = s_in @ W1_0 / np.sqrt(MUL_S)
            v = jnp.einsum('nuc,uv->nvc', v_in, W1_1) / np.sqrt(MUL_V)
            h = jax.nn.silu(edge_attr @ Wfc1 / np.sqrt(NB))
            h = jax.nn.silu(h @ Wfc2 / np.sqrt(NH))
            w = h @ Wfc3 / np.sqrt(NH)
            w0, w1, w2 = (w[:, :64], w[:, 64:128], w[:, 128:160])
            w3, w4 = (w[:, 160:192], w[:, 192:224])
            sd = s[edge_dst]
            vd = v[edge_dst]
            sh0 = edge_sh[:, :1]
            sh1 = edge_sh[:, 1:4]
            m0 = w0 * sd * sh0
            m1 = w3 * jnp.sum(vd * sh1[:, None, :], -1) * INV_SQRT3
            mv0 = (w1 * sd)[:, :, None] * sh1[:, None, :]
            mv1 = w2[:, :, None] * vd * sh0[:, :, None]
            sh1b = jnp.broadcast_to(sh1[:, None, :], vd.shape)
            mv2 = w4[:, :, None] * jnp.cross(vd, sh1b) * INV_SQRT2
            mid_s = jnp.concatenate([m0, m1], -1)
            mid_v = jnp.concatenate([mv0, mv1, mv2], 1)
            ns = jax.ops.segment_sum(mid_s, edge_src, num_segments=N) / np.sqrt(AVG_NEI)
            nv = jax.ops.segment_sum(mid_v, edge_src, num_segments=N) / np.sqrt(AVG_NEI)
            out_s = ns @ W2_0 / np.sqrt(96) + sc_s
            out_v = jnp.einsum('nuc,uv->nvc', nv, W2_1) / np.sqrt(128) + sc_v
            rms_s = jnp.sqrt(jnp.mean(out_s ** 2, -1, keepdims=True) + EPS)
            out_s = out_s / rms_s * g0
            rms_v = jnp.sqrt(jnp.mean(jnp.sum(out_v ** 2, -1), -1) + EPS)
            out_v = out_v / rms_v[:, None, None] * g1[None, :, None]
            return jnp.concatenate([out_s, out_v.reshape(-1, 3 * MUL_V)], -1)
        key = jax.random.key(seed)
        ks = jax.random.split(key, 16)
        inp = {}
        inp['node_hiddens'] = jax.random.normal(ks[0], (N, MUL_S + 3 * MUL_V), jnp.float32)
        inp['edge_index'] = jax.random.randint(ks[1], (2, E), 0, N)
        inp['edge_sh'] = jax.random.normal(ks[2], (E, 4), jnp.float32)
        inp['edge_attr'] = jax.random.uniform(ks[3], (E, NB), jnp.float32)
        inp['W1_0'] = jax.random.normal(ks[4], (MUL_S, MUL_S), jnp.float32)
        inp['W1_1'] = jax.random.normal(ks[5], (MUL_V, MUL_V), jnp.float32)
        inp['Wfc1'] = jax.random.normal(ks[6], (NB, NH), jnp.float32)
        inp['Wfc2'] = jax.random.normal(ks[7], (NH, NH), jnp.float32)
        inp['Wfc3'] = jax.random.normal(ks[8], (NH, WNUM), jnp.float32)
        inp['W2_0'] = jax.random.normal(ks[9], (96, MUL_S), jnp.float32)
        inp['W2_1'] = jax.random.normal(ks[10], (128, MUL_V), jnp.float32)
        inp['Wsc0'] = jax.random.normal(ks[11], (MUL_S, MUL_S), jnp.float32)
        inp['Wsc1'] = jax.random.normal(ks[12], (MUL_V, MUL_V), jnp.float32)
        inp['g0'] = jnp.ones((MUL_S,), jnp.float32)
        inp['g1'] = jnp.ones((MUL_V,), jnp.float32)
        return inp
    _L0_gnn_all = _L0_gnn_setup()
    _L0_gnn_in = {k: v for k, v in _L0_gnn_all.items() if k in ('W1_0', 'W1_1', 'Wfc1', 'Wfc2', 'Wfc3', 'W2_0', 'W2_1', 'Wsc0', 'Wsc1', 'g0', 'g1')}
    del _L0_gnn_all

    def _L1_gnn_setup():
        import jax, jax.numpy as jnp
        import numpy as np
        N, E = (1250, 20000)
        S_IN, V_IN = (64, 32)
        S_MID, V_MID = (96, 128)
        S_OUT, V_OUT = (96, 32)
        R = 64
        FC_HID = 64
        W_NUMEL = 64 + 64 + 32 + 32 + 32
        NUM_NEIGHBORS = 16.0

        def _inv(d):
            return 1.0 / jnp.sqrt(jnp.float32(d))

        def _forward(node_features, node_attr, edge_attr, edge_scalars, lin1_ws, lin1_wv, fc_w1, fc_w2, sc_ws, sc_wv, lin2_ws, lin2_wv, edge_src, edge_dst):
            n = node_features.shape[0]
            s = node_features[:, :S_IN]
            v = node_features[:, S_IN:].reshape(n, V_IN, 3)
            a = node_attr
            sc_s = s @ sc_ws * a * _inv(S_IN)
            sc_v = jnp.einsum('nci,cd->ndi', v, sc_wv) * a[:, :, None] * _inv(V_IN)
            h_s = s @ lin1_ws * a * _inv(S_IN)
            h_v = jnp.einsum('nci,cd->ndi', v, lin1_wv) * a[:, :, None] * _inv(V_IN)
            hid = jax.nn.silu(edge_scalars @ fc_w1 * _inv(R))
            w = hid @ fc_w2 * _inv(FC_HID)
            w1, w2, w3, w4, w5 = jnp.split(w, [64, 128, 160, 192], axis=-1)
            es = h_s[edge_src]
            ev = h_v[edge_src]
            e0 = edge_attr[:, :1]
            e1 = edge_attr[:, 1:4]
            m_s1 = w1 * es * e0
            m_s2 = w4 * jnp.einsum('eci,ei->ec', ev, e1) * _inv(3)
            m_v1 = (w2 * es)[:, :, None] * e1[:, None, :]
            m_v2 = w3[:, :, None] * ev * e0[:, :, None]
            m_v3 = w5[:, :, None] * jnp.cross(ev, e1[:, None, :]) * _inv(2)
            mid_s = jnp.concatenate([m_s1, m_s2], axis=-1)
            mid_v = jnp.concatenate([m_v1, m_v2, m_v3], axis=1)
            inv_nn = 1.0 / jnp.sqrt(jnp.float32(NUM_NEIGHBORS))
            agg_s = jax.ops.segment_sum(mid_s, edge_dst, num_segments=n) * inv_nn
            agg_v = jax.ops.segment_sum(mid_v, edge_dst, num_segments=n) * inv_nn
            o_s = agg_s @ lin2_ws * a * _inv(S_MID)
            o_v = jnp.einsum('nci,cd->ndi', agg_v, lin2_wv) * a[:, :, None] * _inv(V_MID)
            pre_s = sc_s + o_s
            pre_v = sc_v + o_v
            scalars = jax.nn.silu(pre_s[:, :64])
            gates = jax.nn.sigmoid(pre_s[:, 64:96])
            gated = gates[:, :, None] * pre_v
            return jnp.concatenate([scalars, gated.reshape(n, 3 * V_OUT)], axis=-1)
        key = jax.random.key(seed)
        ks = jax.random.split(key, 13)
        return {'node_features': jax.random.normal(ks[0], (N, S_IN + 3 * V_IN), jnp.float32), 'node_attr': jnp.ones((N, 1), jnp.float32), 'edge_src': jax.random.randint(ks[1], (E,), 0, N), 'edge_dst': jax.random.randint(ks[2], (E,), 0, N), 'edge_attr': jax.random.normal(ks[3], (E, 4), jnp.float32), 'edge_scalars': jax.random.normal(ks[4], (E, R), jnp.float32), 'lin1_ws': jax.random.normal(ks[5], (S_IN, S_IN), jnp.float32), 'lin1_wv': jax.random.normal(ks[6], (V_IN, V_IN), jnp.float32), 'fc_w1': jax.random.normal(ks[7], (R, FC_HID), jnp.float32), 'fc_w2': jax.random.normal(ks[8], (FC_HID, W_NUMEL), jnp.float32), 'sc_ws': jax.random.normal(ks[9], (S_IN, S_OUT), jnp.float32), 'sc_wv': jax.random.normal(ks[10], (V_IN, V_OUT), jnp.float32), 'lin2_ws': jax.random.normal(ks[11], (S_MID, S_OUT), jnp.float32), 'lin2_wv': jax.random.normal(ks[12], (V_MID, V_OUT), jnp.float32)}
    _L1_gnn_all = _L1_gnn_setup()
    _L1_gnn_in = {k: v for k, v in _L1_gnn_all.items() if k in ('lin1_ws', 'lin1_wv', 'fc_w1', 'fc_w2', 'sc_ws', 'sc_wv', 'lin2_ws', 'lin2_wv')}
    del _L1_gnn_all
    return {'x': x, 'src': src, 'dst': dst, 'edge_attr_4': edge_attr_4, 'edge_attr_64': edge_attr_64, 'edge_attr_8': edge_attr_8, 'node_vec1': node_vec1, 'L0_gnn_W1_0': _L0_gnn_in['W1_0'], 'L0_gnn_W1_1': _L0_gnn_in['W1_1'], 'L0_gnn_Wfc1': _L0_gnn_in['Wfc1'], 'L0_gnn_Wfc2': _L0_gnn_in['Wfc2'], 'L0_gnn_Wfc3': _L0_gnn_in['Wfc3'], 'L0_gnn_W2_0': _L0_gnn_in['W2_0'], 'L0_gnn_W2_1': _L0_gnn_in['W2_1'], 'L0_gnn_Wsc0': _L0_gnn_in['Wsc0'], 'L0_gnn_Wsc1': _L0_gnn_in['Wsc1'], 'L0_gnn_g0': _L0_gnn_in['g0'], 'L0_gnn_g1': _L0_gnn_in['g1'], 'L1_gnn_lin1_ws': _L1_gnn_in['lin1_ws'], 'L1_gnn_lin1_wv': _L1_gnn_in['lin1_wv'], 'L1_gnn_fc_w1': _L1_gnn_in['fc_w1'], 'L1_gnn_fc_w2': _L1_gnn_in['fc_w2'], 'L1_gnn_sc_ws': _L1_gnn_in['sc_ws'], 'L1_gnn_sc_wv': _L1_gnn_in['sc_wv'], 'L1_gnn_lin2_ws': _L1_gnn_in['lin2_ws'], 'L1_gnn_lin2_wv': _L1_gnn_in['lin2_wv']}

def reference(x, src, dst, edge_attr_4, edge_attr_64, edge_attr_8, node_vec1, L0_gnn_W1_0, L0_gnn_W1_1, L0_gnn_Wfc1, L0_gnn_Wfc2, L0_gnn_Wfc3, L0_gnn_W2_0, L0_gnn_W2_1, L0_gnn_Wsc0, L0_gnn_Wsc1, L0_gnn_g0, L0_gnn_g1, L1_gnn_lin1_ws, L1_gnn_lin1_wv, L1_gnn_fc_w1, L1_gnn_fc_w2, L1_gnn_sc_ws, L1_gnn_sc_wv, L1_gnn_lin2_ws, L1_gnn_lin2_wv):
    import jax
    import jax.numpy as jnp

    def _L0_gnn_ref(node_hiddens, edge_index, edge_sh, edge_attr, W1_0, W1_1, Wfc1, Wfc2, Wfc3, W2_0, W2_1, Wsc0, Wsc1, g0, g1):
        import jax, jax.numpy as jnp
        import numpy as np
        N = 25000
        E = 12500
        MUL_S, MUL_V = (64, 32)
        NB, NH = (8, 64)
        WNUM = 64 + 64 + 32 + 32 + 32
        AVG_NEI = 16.0
        EPS = 1e-05
        INV_SQRT3 = 1.0 / np.sqrt(3.0)
        INV_SQRT2 = 1.0 / np.sqrt(2.0)

        def _split(x):
            return (x[:, :MUL_S], x[:, MUL_S:].reshape(-1, MUL_V, 3))

        def _forward(node_hiddens, edge_sh, edge_attr, W1_0, W1_1, Wfc1, Wfc2, Wfc3, W2_0, W2_1, Wsc0, Wsc1, g0, g1, edge_src, edge_dst):
            s_in, v_in = _split(node_hiddens)
            sc_s = s_in @ Wsc0 / np.sqrt(MUL_S)
            sc_v = jnp.einsum('nuc,uv->nvc', v_in, Wsc1) / np.sqrt(MUL_V)
            s = s_in @ W1_0 / np.sqrt(MUL_S)
            v = jnp.einsum('nuc,uv->nvc', v_in, W1_1) / np.sqrt(MUL_V)
            h = jax.nn.silu(edge_attr @ Wfc1 / np.sqrt(NB))
            h = jax.nn.silu(h @ Wfc2 / np.sqrt(NH))
            w = h @ Wfc3 / np.sqrt(NH)
            w0, w1, w2 = (w[:, :64], w[:, 64:128], w[:, 128:160])
            w3, w4 = (w[:, 160:192], w[:, 192:224])
            sd = s[edge_dst]
            vd = v[edge_dst]
            sh0 = edge_sh[:, :1]
            sh1 = edge_sh[:, 1:4]
            m0 = w0 * sd * sh0
            m1 = w3 * jnp.sum(vd * sh1[:, None, :], -1) * INV_SQRT3
            mv0 = (w1 * sd)[:, :, None] * sh1[:, None, :]
            mv1 = w2[:, :, None] * vd * sh0[:, :, None]
            sh1b = jnp.broadcast_to(sh1[:, None, :], vd.shape)
            mv2 = w4[:, :, None] * jnp.cross(vd, sh1b) * INV_SQRT2
            mid_s = jnp.concatenate([m0, m1], -1)
            mid_v = jnp.concatenate([mv0, mv1, mv2], 1)
            ns = jax.ops.segment_sum(mid_s, edge_src, num_segments=N) / np.sqrt(AVG_NEI)
            nv = jax.ops.segment_sum(mid_v, edge_src, num_segments=N) / np.sqrt(AVG_NEI)
            out_s = ns @ W2_0 / np.sqrt(96) + sc_s
            out_v = jnp.einsum('nuc,uv->nvc', nv, W2_1) / np.sqrt(128) + sc_v
            rms_s = jnp.sqrt(jnp.mean(out_s ** 2, -1, keepdims=True) + EPS)
            out_s = out_s / rms_s * g0
            rms_v = jnp.sqrt(jnp.mean(jnp.sum(out_v ** 2, -1), -1) + EPS)
            out_v = out_v / rms_v[:, None, None] * g1[None, :, None]
            return jnp.concatenate([out_s, out_v.reshape(-1, 3 * MUL_V)], -1)
        edge_src = edge_index[0]
        edge_dst = edge_index[1]
        return _forward(node_hiddens, edge_sh, edge_attr, W1_0, W1_1, Wfc1, Wfc2, Wfc3, W2_0, W2_1, Wsc0, Wsc1, g0, g1, edge_src, edge_dst)

    def _L1_gnn_ref(node_features, node_attr, edge_src, edge_dst, edge_attr, edge_scalars, lin1_ws, lin1_wv, fc_w1, fc_w2, sc_ws, sc_wv, lin2_ws, lin2_wv):
        import jax, jax.numpy as jnp
        import numpy as np
        N, E = (1250, 20000)
        S_IN, V_IN = (64, 32)
        S_MID, V_MID = (96, 128)
        S_OUT, V_OUT = (96, 32)
        R = 64
        FC_HID = 64
        W_NUMEL = 64 + 64 + 32 + 32 + 32
        NUM_NEIGHBORS = 16.0

        def _inv(d):
            return 1.0 / jnp.sqrt(jnp.float32(d))

        def _forward(node_features, node_attr, edge_attr, edge_scalars, lin1_ws, lin1_wv, fc_w1, fc_w2, sc_ws, sc_wv, lin2_ws, lin2_wv, edge_src, edge_dst):
            n = node_features.shape[0]
            s = node_features[:, :S_IN]
            v = node_features[:, S_IN:].reshape(n, V_IN, 3)
            a = node_attr
            sc_s = s @ sc_ws * a * _inv(S_IN)
            sc_v = jnp.einsum('nci,cd->ndi', v, sc_wv) * a[:, :, None] * _inv(V_IN)
            h_s = s @ lin1_ws * a * _inv(S_IN)
            h_v = jnp.einsum('nci,cd->ndi', v, lin1_wv) * a[:, :, None] * _inv(V_IN)
            hid = jax.nn.silu(edge_scalars @ fc_w1 * _inv(R))
            w = hid @ fc_w2 * _inv(FC_HID)
            w1, w2, w3, w4, w5 = jnp.split(w, [64, 128, 160, 192], axis=-1)
            es = h_s[edge_src]
            ev = h_v[edge_src]
            e0 = edge_attr[:, :1]
            e1 = edge_attr[:, 1:4]
            m_s1 = w1 * es * e0
            m_s2 = w4 * jnp.einsum('eci,ei->ec', ev, e1) * _inv(3)
            m_v1 = (w2 * es)[:, :, None] * e1[:, None, :]
            m_v2 = w3[:, :, None] * ev * e0[:, :, None]
            m_v3 = w5[:, :, None] * jnp.cross(ev, e1[:, None, :]) * _inv(2)
            mid_s = jnp.concatenate([m_s1, m_s2], axis=-1)
            mid_v = jnp.concatenate([m_v1, m_v2, m_v3], axis=1)
            inv_nn = 1.0 / jnp.sqrt(jnp.float32(NUM_NEIGHBORS))
            agg_s = jax.ops.segment_sum(mid_s, edge_dst, num_segments=n) * inv_nn
            agg_v = jax.ops.segment_sum(mid_v, edge_dst, num_segments=n) * inv_nn
            o_s = agg_s @ lin2_ws * a * _inv(S_MID)
            o_v = jnp.einsum('nci,cd->ndi', agg_v, lin2_wv) * a[:, :, None] * _inv(V_MID)
            pre_s = sc_s + o_s
            pre_v = sc_v + o_v
            scalars = jax.nn.silu(pre_s[:, :64])
            gates = jax.nn.sigmoid(pre_s[:, 64:96])
            gated = gates[:, :, None] * pre_v
            return jnp.concatenate([scalars, gated.reshape(n, 3 * V_OUT)], axis=-1)
        return _forward(node_features, node_attr, edge_attr, edge_scalars, lin1_ws, lin1_wv, fc_w1, fc_w2, sc_ws, sc_wv, lin2_ws, lin2_wv, edge_src, edge_dst)
    edge_index = jnp.stack([src, dst])
    x = _layernorm(x + _L0_gnn_ref(x, edge_index, edge_attr_4, edge_attr_8, L0_gnn_W1_0, L0_gnn_W1_1, L0_gnn_Wfc1, L0_gnn_Wfc2, L0_gnn_Wfc3, L0_gnn_W2_0, L0_gnn_W2_1, L0_gnn_Wsc0, L0_gnn_Wsc1, L0_gnn_g0, L0_gnn_g1), axis=-1)
    x = _layernorm(x + _L1_gnn_ref(x, node_vec1, src, dst, edge_attr_4, edge_attr_64, L1_gnn_lin1_ws, L1_gnn_lin1_wv, L1_gnn_fc_w1, L1_gnn_fc_w2, L1_gnn_sc_ws, L1_gnn_sc_wv, L1_gnn_lin2_ws, L1_gnn_lin2_wv), axis=-1)
    return x

_drawn_inputs = setup_inputs


def setup_inputs(seed=0):
    import zlib

    import numpy as np

    out = dict(_drawn_inputs(seed))
    spreads = {'L0_gnn_g0': (1.0, 0.2), 'L0_gnn_g1': (1.0, 0.2)}
    factors = {'edge_attr_8': 4.175,
     'L0_gnn_W1_1': 3.548,
     'L0_gnn_W2_0': 2.73,
     'L0_gnn_W2_1': 3.233,
     'L1_gnn_lin1_wv': 3.653,
     'L1_gnn_lin2_ws': 3.112,
     'L1_gnn_lin2_wv': 2.997}
    for name, (base, spread) in spreads.items():
        noise = np.random.default_rng([zlib.crc32(name.encode()), seed]).standard_normal(out[name].shape)
        drawn = base * np.exp(spread * noise) if base else spread * noise
        out[name] = jnp.asarray(drawn.astype(out[name].dtype))
    for name, factor in factors.items():
        out[name] = (out[name] * factor).astype(out[name].dtype)
    return out
```

```python
from contextlib import ExitStack

import concourse.bass as bass
import concourse.mybir as mybir
from concourse.alu_op_type import AluOpType as ALU

ACT = mybir.ActivationFunctionType
F32 = mybir.dt.float32
I32 = mybir.dt.int32
AX_X = mybir.AxisListType.X

P = 128
TILES = 4
ROWS = P * TILES
N_NODES = 25000
GROUPS = -(-N_NODES // ROWS)
N_PAD = GROUPS * ROWS
COLS = GROUPS * TILES
TABLES = 2
S_IN, V_IN, XYZ = 64, 32, 3
V3 = V_IN * XYZ
F_IN = S_IN + V3
HID = 64
W_ALL = 2 * S_IN + 3 * V_IN
OUT_S = (64, 96)
ATTR = (8, 64)
SLOT = 256
BANK = 512
EPS = 1e-5
NEIGHBOURS = 16.0
HIDDEN_SCALE = (ATTR[0] ** -0.5, ATTR[1] ** -0.5)

def _columns(widths):
    at, out = 0, {}
    for name, n in widths:
        out[name] = (at, at + n)
        at += n
    return out, at


WEIGHT_COLS, WEIGHT_WIDTH = _columns([
    ("node_s0", 64 + 64), ("node_v0", 2 * V3), ("node_s1", 96 + 64), ("node_v1", 2 * V3),
    ("fc1_0", HID), ("fc2_0", HID), ("edge_w0", W_ALL), ("fc1_1", HID), ("edge_w1", W_ALL),
    ("outA0", V_IN + 64), ("outB0", 64 + V3), ("outC0", V3),
    ("outA1", V_IN + 96), ("outB1", 96 + V3), ("outC1", V3)])


class Group:

    def __init__(self, half, parity):
        self.half, self.parity = half, parity
        self.index = 2 * half + parity
        self.static = isinstance(half, int)
        self.reuses = not (self.static and half == 0)
        self.is_first = self.static and self.index == 0
        self.is_last = self.static and self.index == GROUPS - 1

    def next(self):
        return Group(self.half + self.parity, 1 - self.parity)

    def prev(self):
        return Group(self.half - 1 + self.parity, 1 - self.parity)

    def done(self, layer=0):
        return layer * GROUPS + self.index + 1

    def uses(self, layer=0):
        return layer * ((GROUPS + 1 - self.parity) // 2) + self.half + 1


def walk(eng, step):
    for first in range(4):
        step(Group(first // 2, first % 2))
    with eng.Fori(2, GROUPS // 2) as i:
        step(Group(i, 0))
        step(Group(i, 1))
    step(Group(GROUPS // 2, 0))


def build(nc, t, out):
    ctx = ExitStack()
    with ctx:
        def sb(name, shape, dt=F32):
            return ctx.enter_context(nc.sbuf_tensor(name, shape, dt))

        def ps(name, shape):
            return ctx.enter_context(nc.psum_tensor(name, shape, F32))

        def sem(name):
            return ctx.enter_context(nc.semaphore(name))

        def sem2(name):
            return [sem(f"{name}{b}") for b in range(2)]

        def dram(name, shape):
            return nc.dram_tensor(name, shape, F32).ap()

        h_tab = [dram("h_tab0", (N_PAD, F_IN)), dram("h_tab1", (N_PAD, F_IN))]
        ACC_W = [OUT_S[0] + V3, OUT_S[1] + V3]
        acc_tab = [[dram(f"acc_tab{l}{k}", (N_PAD + P, ACC_W[l])) for k in range(TABLES)] for l in range(2)]
        x1_tab = dram("x1_tab", (N_PAD, F_IN))

        def rows(tab, g):
            r0 = g.index * ROWS
            return tab[bass.ds(r0, ROWS), :].rearrange("(p j) f -> p (j f)", j=TILES)

        W = sb("W", [P, WEIGHT_WIDTH])
        ident = sb("ident", [P, P])
        before = sb("before", [P, P])
        gain = sb("gain", [P, F_IN])
        eps = sb("eps", [P, 1])
        dump_row = sb("dump_row", [P, 1])
        zeros = sb("zeros", [P, TILES * ACC_W[1]])
        idx_i = [sb("src_i", [P, COLS], I32), sb("dst_i", [P, COLS], I32)]
        idx_f = [sb("src_f", [P, COLS]), sb("dst_f", [P, COLS])]
        repeats = sb("repeats", [P, 2, COLS])
        to_dump = sb("to_dump", [P, 2, COLS])
        add_row = [sb("add_row0", [P, COLS], I32), sb("add_row1", [P, COLS], I32)]
        sh = sb("sh", [P, COLS, 5])
        node_a = sb("node_a", [P, COLS])
        read_now = sb("read_now", [P, 2, TILES], I32)
        add_now = sb("add_now", [P, 2, TILES], I32)
        read_now_ready, add_now_ready = sem("read_now_ready"), sem("add_now_ready")

        def weight(name, p0, p1):
            c0, c1 = WEIGHT_COLS[name]
            return W[p0:p1, c0:c1]

        idx_row = sb("idx_row", [P, 2, 2, ROWS], I32)
        xs = sb("xs", [S_IN, 2, ROWS])
        xv = sb("xv", [V3, 2, ROWS])
        sc_sb = sb("sc_sb", [P, 2, TILES, ACC_W[1]])
        h_sb = sb("h_sb", [P, 2, TILES, F_IN])
        junk = sb("junk", [P, 2, TILES, P])

        hg = sb("hg", [P, 2, TILES, F_IN])
        attr = sb("attr", [HID, 2, ROWS])
        hidden = sb("hidden", [P, ROWS])
        U = sb("U", [P, 2, TILES, 288])
        crossed = sb("crossed", [P, TILES, V3])
        prod = sb("prod", [P, TILES, 352])
        prodT = sb("prodT", [P, 3, ROWS])
        same = sb("same", [P, 2, TILES, P])
        pw_sb = sb("pw_sb", [P, TILES, V_IN])
        spread = sb("spread", [P, TILES, V3])
        msg = sb("msg", [P, TILES, ACC_W[1]])
        merged = sb("merged", [P, 2, TILES, ACC_W[1]])

        accs = sb("accs", [P, 2, TABLES, TILES * ACC_W[1]])
        xin = sb("xin", [P, 2, TILES, F_IN])
        y = sb("y", [P, TILES, F_IN])
        pre = sb("pre", [P, TILES, ACC_W[1]])
        sq = sb("sq", [P, TILES, F_IN])
        ms = sb("ms", [P, 2, TILES])
        rms = sb("rms", [P, 2, TILES])
        stats = sb("stats", [P, TILES, 6])
        mv = sb("mv", [P, TILES, 2])
        std = sb("std", [P, TILES])
        x1 = sb("x1", [P, 2, TILES, F_IN])

        psum = ps("psum", [P, 8 * BANK])

        consts_ready, weights_in, weights_zero, weights_ready = (
            sem("consts_ready"), sem("weights_in"), sem("weights_zero"), sem("weights_ready"))
        tables_in = sem("tables_in")
        idx_float, phase_end = sem("idx_float"), sem("phase_end")
        xT_in, idx_row_in = sem2("xT_in"), sem2("idx_row_in")
        node_mm, sc_evac, h_evac = sem("node_mm"), sem("sc_evac"), sem("h_evac")
        sc_out, h_out, zero_out = sem2("sc_out"), sem2("h_out"), sem("zero_out")
        counted, add_step = sem("counted"), sem("add_step")

        attr_in, hg_in = sem2("attr_in"), sem2("hg_in")
        h1_mm, h1_act, h2_mm, h2_act, w_mm = (sem("h1_mm"), sem("h1_act"), sem("h2_mm"), sem("h2_act"), sem("w_mm"))
        u_dot, u_ready = sem("u_dot"), sem("u_ready")
        prod_ready, prod_tr, prodT_ready = sem("prod_ready"), sem("prod_tr"), sem("prodT_ready")
        out_mm, pw_ready, s_ready, spread_ready, msg_ready = (
            sem("out_mm"), sem("pw_ready"), sem("s_ready"), sem("spread_ready"), sem("msg_ready"))
        same_ready, merge_mm = sem("same_ready"), sem("merge_mm")
        added = [sem(f"added{k}") for k in range(TABLES)]

        acc_in, x_in, x1_out = sem2("acc_in"), sem2("x_in"), sem2("x1_out")
        node_chain, prod_part, merged_half = sem("node_chain"), sem("prod_part"), sem("merged_half")
        sig = sb("sig", [P, TILES, OUT_S[1]])
        sq_ready, rms_ready, std_ready = sem("sq_ready"), sem("rms_ready"), sem("std_ready")
        ms_ready, var_ready, x1_ready = sem("ms_ready"), sem("var_ready"), sem("x1_ready")
        x1_tr, x1T_ready = sem("x1_tr"), sem("x1T_ready")
        y_ready, sig_ready = sem("y_ready"), sem("sig_ready")

        ENGINES = 5

        def next_phase(eng, k):
            eng.drain().then_inc(phase_end, 1)
            eng.wait_ge(phase_end, ENGINES * k)

        waits_held = sem("waits_held")

        def hold(eng):
            eng.sem_inc(waits_held, 1)

        def blocks(name, p0, c0, src):
            first = WEIGHT_COLS[name][0]
            return [(W[p0 + V_IN * c:p0 + V_IN * (c + 1), first + c0 + V_IN * c:first + c0 + V_IN * (c + 1)], src)
                    for c in range(XYZ)]

        def part(name, p0, p1, c0, c1, src):
            first = WEIGHT_COLS[name][0]
            return [(W[p0:p1, first + c0:first + c1], src)]

        weight_dmas = []
        for l in range(2):
            sc, scv, lin, linv = t[f"sc_s{l}"], t[f"sc_v{l}"], t[f"lin_s{l}"], t[f"lin_v{l}"]
            os_ = OUT_S[l]
            weight_dmas += part(f"node_s{l}", 0, S_IN, 0, os_, sc)
            weight_dmas += part(f"node_s{l}", 0, S_IN, os_, os_ + S_IN, lin)
            weight_dmas += blocks(f"node_v{l}", 0, 0, scv) + blocks(f"node_v{l}", 0, V3, linv)
            fc, q0 = t[f"fc_w{l}"], HID * (1 - l)
            for c0, c1, f0 in ((0, 64, 64), (64, 128, 0), (128, W_ALL, 128)):
                weight_dmas += part(f"edge_w{l}", q0, q0 + HID, c0, c1, fc[:, f0:f0 + c1 - c0])
            o_s, o_v = t[f"out_s{l}"], t[f"out_v{l}"]
            weight_dmas += part(f"outA{l}", 0, 64, 0, V_IN, o_v[0:64, :])
            weight_dmas += part(f"outA{l}", 64, 128, V_IN, V_IN + os_, o_s[0:64, :])
            weight_dmas += part(f"outB{l}", V3, P, 0, os_, o_s[64:96, :])
            weight_dmas += blocks(f"outB{l}", 0, os_, o_v[64:96, :]) + blocks(f"outC{l}", 0, 0, o_v[96:128, :])
        weight_dmas += part("fc1_0", 0, ATTR[0], 0, HID, t["fc1_0"])
        weight_dmas += part("fc2_0", 0, HID, 0, HID, t["fc2_0"])
        weight_dmas += part("fc1_1", 0, HID, 0, HID, t["fc1_1"])

        scales = []
        for l in range(2):
            def cols(name, a, b):
                c = WEIGHT_COLS[name][0]
                return (c + a, c + b)
            os_ = OUT_S[l]
            f_s = (96 * NEIGHBOURS) ** -0.5
            f_v = (128 * NEIGHBOURS) ** -0.5
            scales += [(cols(f"node_s{l}", 0, os_ + S_IN), S_IN ** -0.5), (cols(f"node_v{l}", 0, 2 * V3), V_IN ** -0.5),
                       (cols(f"edge_w{l}", 0, 160), HID ** -0.5),
                       (cols(f"edge_w{l}", 160, 192), (HID * 3) ** -0.5),
                       (cols(f"edge_w{l}", 192, 224), (HID * 2) ** -0.5),
                       (cols(f"outA{l}", 0, V_IN), f_v), (cols(f"outA{l}", V_IN, V_IN + os_), f_s),
                       (cols(f"outB{l}", 0, os_), f_s), (cols(f"outB{l}", os_, os_ + V3), f_v),
                       (cols(f"outC{l}", 0, V3), f_v)]

        def node_psum(base, j, a, b):
            return psum[:, (base + j) * BANK + a:(base + j) * BANK + b]

        def node_psum4(base, a, b):
            return psum[:, base * BANK:(base + TILES) * BANK].rearrange("p (j c) -> p j c", j=TILES)[:, :, a:b]

        H1_PS = psum[0:HID, 0:BANK]
        H2_PS = psum[HID:P, 0:BANK]
        W_PS = psum[:, BANK:3 * BANK].rearrange("p (j c) -> p j c", c=SLOT)
        T_PS = [psum[:, 3 * BANK:4 * BANK], psum[:, 4 * BANK:5 * BANK]]
        O_PS = psum[:, 5 * BANK:7 * BANK].rearrange("p (j c) -> p j c", c=SLOT)
        M_PS = psum[:, 7 * BANK:8 * BANK].rearrange("p (j c) -> p j c", c=SLOT)
        CHUNKS = ((0, 128), (128, 256), (256, 352))

        block = ctx.enter_context(nc.Block())

        @block.sync
        def _(sp):
            for k in range(2):
                sp.dma_start(idx_i[k][:], t[("src", "dst")[k] + "_cols"][:]).then_inc(tables_in, 16)
            sp.dma_start(sh[:], t["sh"].rearrange("p (c k) -> p c k", k=5)).then_inc(tables_in, 16)
            sp.dma_start(node_a[:], t["node_a"]).then_inc(tables_in, 16)
            sp.dma_start(gain[:], t["gain"].partition_broadcast(P)).then_inc(tables_in, 16)
            sp.wait_ge(weights_zero, 1)
            for dst, src in weight_dmas:
                sp.dma_start(dst, src).then_inc(weights_in, 16)

            def load_nodes(g):
                b = g.parity
                if g.reuses:
                    sp.wait_ge(node_mm, g.done() - 2)
                sp.dma_start(xs[:, b, :], t["xT"][g.index, 0:S_IN, :]).then_inc(xT_in[b], 16)
                sp.dma_start(xv[:, b, :], t["xT"][g.index, S_IN:F_IN, :]).then_inc(xT_in[b], 16)
                if g.reuses:
                    sp.wait_ge(counted, 2 * TILES * (g.done() - 2))
                for k in range(2):
                    sp.dma_start(idx_row[:, b, k, :], t[("src", "dst")[k] + "_rows"][g.index, :].partition_broadcast(P)) \
                        .then_inc(idx_row_in[b], 16)
            walk(sp, load_nodes)
            next_phase(sp, 1)

            def load_edges(layer):
                k_add = ("src", "dst")[layer] + "_rows"

                def step(g):
                    b = g.parity
                    if g.reuses:
                        sp.wait_ge(h1_mm, g.done(layer) - 2)
                        sp.wait_ge(same_ready, g.done(layer) - 2)
                    sp.dma_start(attr[0:ATTR[layer], b, :], t[f"attrT{layer}"][g.index]).then_inc(attr_in[b], 16)
                    sp.dma_start(idx_row[:, b, 0, :], t[k_add][g.index, :].partition_broadcast(P)) \
                        .then_inc(attr_in[b], 16)
                walk(sp, step)

            def load_sums(layer, x_src):
                w = ACC_W[layer]

                def step(g):
                    b = g.parity
                    if g.reuses:
                        sp.wait_ge(x1_ready, g.done(layer) - 2)
                    for k in range(TABLES):
                        sp.dma_start(accs[:, b, k, 0:TILES * w], rows(acc_tab[layer][k], g)).then_inc(acc_in[b], 16)
                    sp.dma_start(xin[:, b, :, :].rearrange("p j f -> p (j f)"), rows(x_src, g)).then_inc(x_in[b], 16)
                walk(sp, step)

            load_edges(0)
            next_phase(sp, 2)
            load_sums(0, t["x"])
            next_phase(sp, 3)
            load_edges(1)
            next_phase(sp, 4)
            load_sums(1, x1_tab)
            next_phase(sp, 5)

        @block.gpsimd
        def _(pool):
            pool.memset(W[:], 0.0).then_inc(weights_zero, 1)
            pool.memset(ident[:], 0.0).then_inc(consts_ready, 1)
            pool.memset(before[:], 1.0).then_inc(consts_ready, 1)
            pool.memset(eps[:], EPS).then_inc(consts_ready, 1)
            pool.memset(zeros[:], 0.0).then_inc(consts_ready, 1)
            pool.iota(dump_row[:], pattern=[[0, 1]], base=N_PAD, channel_multiplier=1,
                      allow_small_or_imprecise_dtypes=True).then_inc(consts_ready, 1)
            pool.wait_ge(consts_ready, 5)
            pool.affine_select(out=ident[:], in_=ident[:], compare_op=ALU.not_equal, fill=1.0, base=0,
                               pattern=[[-1, P]], channel_multiplier=1).then_inc(consts_ready, 1)
            pool.affine_select(out=before[:], in_=before[:], compare_op=ALU.is_gt, fill=0.0, base=0,
                               pattern=[[-1, P]], channel_multiplier=1).then_inc(consts_ready, 1)

            next_phase(pool, 1)

            def edges(layer):
                gather_by = idx_i[1 - layer]
                w = ACC_W[layer]

                def gather(g):
                    b = g.parity
                    if g.reuses:
                        pool.wait_ge(prod_ready, g.done(layer) - 2)
                        pool.wait_ge(u_ready, g.done(layer) - 2)
                    pool.tensor_copy(read_now[:, b, :], gather_by[:, bass.ds(g.index * TILES, TILES)]) \
                        .then_inc(read_now_ready, 1)
                    pool.wait_ge(read_now_ready, g.done(layer))
                    hold(pool)
                    for j in range(TILES):
                        pool.indirect_dma_start(
                            out=hg[:, b, j, :], out_offset=None, in_=h_tab[layer][:, :],
                            in_offset=bass.IndirectOffsetOnAxis(ap=read_now[:, b, j:j + 1], axis=0)) \
                            .then_inc(hg_in[b], 16)

                def scatter(g):
                    b = g.parity
                    pool.tensor_copy(add_now[:, b, :], add_row[layer][:, bass.ds(g.index * TILES, TILES)]) \
                        .then_inc(add_now_ready, 1)
                    for j in range(TILES):
                        pool.wait_ge(add_now_ready, g.done(layer))
                        pool.wait_ge(merged_half, 2 * (g.done(layer) - 1) + j // 2 + 1)
                        k = j % TABLES
                        before_this = (layer * COLS + g.index * TILES + j) // TABLES if g.static else \
                            (layer * COLS // TABLES + g.index * (TILES // TABLES) + j // TABLES)
                        if not g.static or before_this:
                            pool.wait_ge(added[k], 16 * before_this)
                            hold(pool)
                        pool.indirect_dma_start(
                            out=acc_tab[layer][k][:, :],
                            out_offset=bass.IndirectOffsetOnAxis(ap=add_now[:, b, j:j + 1], axis=0),
                            in_=merged[:, b, j, 0:w], in_offset=None, compute_op=ALU.add).then_inc(added[k], 16)

                gather(Group(0, 0))

                def step(g):
                    if not g.is_last:
                        gather(g.next())
                    if not g.is_first:
                        scatter(g.prev())
                walk(pool, step)
                scatter(Group(GROUPS // 2, 0))
                for k in range(TABLES):
                    pool.wait_ge(added[k], 16 * (layer + 1) * COLS // TABLES)

            edges(0)
            next_phase(pool, 2)
            next_phase(pool, 3)
            edges(1)
            next_phase(pool, 4)
            next_phase(pool, 5)

        @block.scalar
        def _(act):
            act.wait_ge(consts_ready, 7)
            for l in range(2):
                for k in range(TABLES):
                    act.dma_start(acc_tab[l][k][N_PAD:N_PAD + P, :], zeros[:, 0:ACC_W[l]]).then_inc(zero_out, 16)

            def project_out(layer, g, base):
                b, w = g.parity, ACC_W[layer]
                act.wait_ge(node_mm, g.done(layer))
                if g.reuses:
                    act.wait_ge(sc_out[b], 16 * (g.uses(layer) - 1))
                sc_buf = sc_sb[:, b].rearrange("p j f -> p (j f)")[:, 0:TILES * w]
                act.activation(sc_buf.rearrange("p (j f) -> p j f", j=TILES), node_psum4(base, 0, w),
                               ACT.Copy).then_inc(sc_evac, 1)
                act.wait_ge(sc_evac, g.done(layer))
                act.dma_start(rows(acc_tab[layer][0], g), sc_buf).then_inc(sc_out[b], 16)
                for k in range(1, TABLES):
                    act.dma_start(rows(acc_tab[layer][k], g), zeros[:, 0:TILES * w]).then_inc(zero_out, 16)
                act.wait_ge(h_evac, g.done(layer))
                act.dma_start(rows(h_tab[layer], g), h_sb[:, b].rearrange("p j f -> p (j f)")).then_inc(h_out[b], 16)

            def stores_landed(layer):
                for b in range(2):
                    last = (layer + 1) * ((GROUPS + 1 - b) // 2)
                    act.wait_ge(sc_out[b], 16 * last)
                    act.wait_ge(h_out[b], 16 * last)
                act.wait_ge(zero_out, 16 * (2 * TABLES + (layer + 1) * GROUPS * (TABLES - 1)))

            walk(act, lambda g: project_out(0, g, TILES * g.parity))
            stores_landed(0)
            next_phase(act, 1)

            def edges(layer):
                os_, w = OUT_S[layer], ACC_W[layer]

                def first_silu(g):
                    n = g.done(layer)
                    act.wait_ge(h1_mm, n)
                    act.activation(hidden[0:HID, :], H1_PS, ACT.Silu, scale=HIDDEN_SCALE[layer]).then_inc(h1_act, 1)

                def second_silu(g):
                    act.wait_ge(h2_mm, g.done(0))
                    act.activation(hidden[HID:P, :], H2_PS, ACT.Silu, scale=HID ** -0.5).then_inc(h2_act, 1)

                def turned_out(g, c):
                    n3 = 3 * (g.done(layer) - 1) + c + 1
                    n_rows = CHUNKS[c][1] - CHUNKS[c][0]
                    act.wait_ge(prod_tr, n3)
                    act.activation(prodT[0:n_rows, c, :], T_PS[c % 2][0:n_rows, :], ACT.Copy).then_inc(prodT_ready, 1)

                def merged_out(g):
                    b = g.parity
                    if g.reuses:
                        for k in range(TABLES):
                            base = layer * COLS // TABLES
                            act.wait_ge(added[k], 16 * (base + (g.index - 1) * (TILES // TABLES)))
                    for q in range(2):
                        act.wait_ge(merge_mm, 2 * (g.done(layer) - 1) + q + 1)
                        act.activation(merged[:, b, 2 * q:2 * q + 2, 0:w], M_PS[:, :, 0:w], ACT.Copy) \
                            .then_inc(merged_half, 1)

                def message_out(g):
                    n = g.done(layer)
                    act.wait_ge(out_mm, n)
                    if not g.is_first:
                        act.wait_ge(spread_ready, n - 1)
                    act.activation(pw_sb[:], O_PS[:, :, 0:V_IN], ACT.Copy).then_inc(pw_ready, 1)
                    if not g.is_first:
                        act.wait_ge(merge_mm, 2 * (n - 1))
                    act.activation(msg[:, :, 0:os_], O_PS[:, :, V_IN:V_IN + os_], ACT.Copy).then_inc(s_ready, 1)

                first_silu(Group(0, 0))
                if layer == 0:
                    second_silu(Group(0, 0))

                def step(g):
                    if not g.is_last:
                        first_silu(g.next())
                    for c in range(3):
                        turned_out(g, c)
                    if layer == 0 and not g.is_last:
                        second_silu(g.next())
                    if not g.is_first:
                        merged_out(g.prev())
                    message_out(g)
                walk(act, step)
                merged_out(Group(GROUPS // 2, 0))

            edges(0)
            next_phase(act, 2)

            def mean_squares(g):
                n = g.done(0)
                act.wait_ge(y_ready, n)
                act.activation(sq[:], y[:], ACT.Square).then_inc(sq_ready, 1)
                act.wait_ge(ms_ready, n)
                act.activation(rms[:, 0, :], ms[:, 0, :], ACT.Sqrt, bias=eps[:, 0:1], scale=1.0 / S_IN)
                act.activation(rms[:, 1, :], ms[:, 1, :], ACT.Sqrt, bias=eps[:, 0:1], scale=1.0 / V_IN) \
                    .then_inc(rms_ready, 1)

            def deviation(layer, g):
                act.wait_ge(var_ready, g.done(layer))
                act.activation(std[:], mv[:, :, 1], ACT.Sqrt, bias=eps[:, 0:1], scale=1.0).then_inc(std_ready, 1)
                act.wait_ge(x1_ready, g.done(layer))
                dst = x1_tab if layer == 0 else out
                act.dma_start(rows(dst, g), x1[:, g.parity].rearrange("p j f -> p (j f)")).then_inc(x1_out[g.parity], 16)

            def nodes0(g):
                mean_squares(g)
                deviation(0, g)
                n = g.done(0)
                act.wait_ge(x1_tr, n)
                act.activation(xs[:, 0, :], psum[0:S_IN, 0:BANK], ACT.Copy)
                act.activation(xv[:, 0, :], psum[0:V3, BANK:2 * BANK], ACT.Copy).then_inc(x1T_ready, 1)
                project_out(1, g, 2)
            walk(act, nodes0)
            stores_landed(1)
            for b in range(2):
                act.wait_ge(x1_out[b], 16 * ((GROUPS + 1 - b) // 2))
            next_phase(act, 3)
            edges(1)
            next_phase(act, 4)

            def nodes1(g):
                act.wait_ge(y_ready, g.done(1))
                act.activation(sig[:], pre[:, :, 0:OUT_S[1]], ACT.Sigmoid).then_inc(sig_ready, 1)
                deviation(1, g)
            walk(act, nodes1)
            for b in range(2):
                act.wait_ge(x1_out[b], 16 * 2 * ((GROUPS + 1 - b) // 2))
            next_phase(act, 5)

        @block.vector
        def _(dve):
            chain = [0]
            dve.wait_ge(weights_in, 16 * len(weight_dmas))
            for (c0, c1), f in scales:
                dve.tensor_scalar(W[:, c0:c1], W[:, c0:c1], f, None, ALU.mult).then_inc(weights_ready, 1)
            dve.wait_ge(tables_in, 16 * 5)
            dve.wait_ge(consts_ready, 7)
            for k in range(2):
                dve.tensor_copy(idx_f[k][:], idx_i[k][:]).then_inc(idx_float, 1)
            dve.wait_ge(idx_float, 2)

            def node_features(g):
                b = g.parity
                dve.wait_ge(node_mm, g.done())
                if g.reuses:
                    dve.wait_ge(h_out[b], 16 * (g.uses() - 1))
                dve.wait_ge(sc_evac, g.done())
                dve.tensor_copy(h_sb[:, b], node_psum4(TILES * b, ACC_W[0], ACC_W[0] + F_IN)).then_inc(h_evac, 1)
                dve.wait_ge(idx_row_in[b], 32 * g.uses())
                if not g.is_first:
                    dve.wait_ge(counted, 2 * TILES * (g.done() - 1))
                for k in range(2):
                    for j in range(TILES):
                        col = g.index * TILES + j
                        dve.scalar_tensor_tensor(
                            out=junk[:, k, j, :], in0=idx_row[:, b, k, j * P:(j + 1) * P],
                            scalar=idx_f[k][:, bass.ds(col, 1)], in1=before[:], op0=ALU.is_equal, op1=ALU.mult,
                            accum_out=repeats[:, k, bass.ds(col, 1)]).then_inc(counted, 1)
            walk(dve, node_features)
            dve.wait_ge(counted, 2 * TILES * GROUPS)

            def link(ins):
                chain[0] += 1
                ins.then_inc(add_step, 1)
                dve.wait_ge(add_step, chain[0])

            for k in range(2):
                link(dve.tensor_scalar(to_dump[:, k], idx_f[k][:], -1.0, dump_row[:, 0:1], ALU.mult, ALU.add))
                link(dve.tensor_scalar(repeats[:, k], repeats[:, k], 1.0, None, ALU.min))
                link(dve.tensor_tensor(to_dump[:, k], to_dump[:, k], repeats[:, k], ALU.mult))
                link(dve.tensor_tensor(add_row[k][:], to_dump[:, k], idx_f[k][:], ALU.add))
            next_phase(dve, 1)

            def edges(layer):
                os_, w = OUT_S[layer], ACC_W[layer]

                def edge_sh(g, k, n, width):
                    v = sh[:, bass.ds(g.index * TILES, TILES), k:k + n]
                    return v.unsqueeze(3).broadcast_to([P, TILES, n, width])

                def directions(g):
                    b, n = g.parity, g.done(layer)
                    s, v = hg[:, b, :, 0:S_IN], hg[:, b, :, S_IN:F_IN].rearrange("p j (c u) -> p j c u", c=XYZ)
                    cross = U[:, b, :, 192:288].rearrange("p j (c u) -> p j c u", c=XYZ)
                    other = crossed[:].rearrange("p j (c u) -> p j c u", c=XYZ)
                    dve.wait_ge(hg_in[b], 16 * TILES * g.uses(layer))
                    dve.tensor_tensor(U[:, b, :, 0:F_IN], hg[:, b], edge_sh(g, 0, 1, F_IN)[:, :, 0, :], ALU.mult)
                    dve.tensor_tensor(cross[:, :, 0:2], v[:, :, 1:3], edge_sh(g, 3, 2, V_IN), ALU.mult)
                    dve.tensor_tensor(cross[:, :, 2:3], v[:, :, 0:1], edge_sh(g, 2, 1, V_IN), ALU.mult)
                    dve.tensor_tensor(other[:, :, 1:3], v[:, :, 0:2], edge_sh(g, 3, 2, V_IN), ALU.mult)
                    dve.tensor_tensor(other[:, :, 0:1], v[:, :, 2:3], edge_sh(g, 2, 1, V_IN), ALU.mult) \
                        .then_inc(u_dot, 1)
                    dve.wait_ge(u_dot, 4 * (n - 1) + 1)
                    dve.tensor_tensor(cross, cross, other, ALU.subtract).then_inc(u_dot, 1)
                    dve.wait_ge(u_dot, 4 * (n - 1) + 2)
                    dve.tensor_tensor(other, v, edge_sh(g, 1, 3, V_IN), ALU.mult).then_inc(u_dot, 1)
                    dve.wait_ge(u_dot, 4 * (n - 1) + 3)
                    dot = U[:, b, :, 160:192]
                    dve.tensor_tensor(dot, other[:, :, 0], other[:, :, 1], ALU.add).then_inc(u_dot, 1)
                    dve.wait_ge(u_dot, 4 * n)
                    dve.tensor_tensor(dot, dot, other[:, :, 2], ALU.add).then_inc(u_ready, 1)

                def same_rows(g):
                    b, n = g.parity, g.done(layer)
                    dve.wait_ge(attr_in[b], 32 * g.uses(layer))
                    if g.reuses:
                        dve.wait_ge(merge_mm, 2 * (n - 2))
                    own = idx_f[layer][:, bass.ds(g.index * TILES, TILES)].unsqueeze(2).broadcast_to([P, TILES, P])
                    dve.tensor_tensor(same[:, b], idx_row[:, b, 0, :].rearrange("p (j q) -> p j q", j=TILES), own,
                                      ALU.is_equal).then_inc(same_ready, 1)

                def products(g):
                    b, n = g.parity, g.done(layer)
                    dve.wait_ge(w_mm, n)
                    dve.wait_ge(u_ready, n)
                    dve.tensor_tensor(prod[:, :, 0:64], W_PS[:, :, 0:64], hg[:, b, :, 0:S_IN], ALU.mult)
                    dve.tensor_tensor(prod[:, :, 64:128], W_PS[:, :, 64:128], U[:, b, :, 0:64], ALU.mult) \
                        .then_inc(prod_part, 1)

                    def spread_w(c0):
                        return W_PS[:, :, c0:c0 + V_IN].unsqueeze(2).broadcast_to([P, TILES, XYZ, V_IN])

                    def xyz(ap):
                        return ap.rearrange("p j (c u) -> p j c u", c=XYZ)
                    dve.tensor_tensor(xyz(prod[:, :, 128:224]), spread_w(128), xyz(U[:, b, :, 64:160]), ALU.mult)
                    dve.tensor_tensor(prod[:, :, 224:256], W_PS[:, :, 160:192], U[:, b, :, 160:192], ALU.mult) \
                        .then_inc(prod_part, 1)
                    dve.tensor_tensor(xyz(prod[:, :, 256:352]), spread_w(192), xyz(U[:, b, :, 192:288]), ALU.mult) \
                        .then_inc(prod_ready, 1)

                def messages(g):
                    n = g.done(layer)
                    dve.wait_ge(pw_ready, n)
                    pw = pw_sb[:].unsqueeze(2).broadcast_to([P, TILES, XYZ, V_IN])
                    dve.tensor_tensor(spread[:].rearrange("p j (c u) -> p j c u", c=XYZ), pw,
                                      edge_sh(g, 1, 3, V_IN), ALU.mult).then_inc(spread_ready, 1)
                    dve.wait_ge(spread_ready, n)
                    dve.wait_ge(s_ready, n)
                    if not g.is_first:
                        dve.wait_ge(merge_mm, 2 * (n - 1))
                    dve.tensor_tensor(msg[:, :, os_:w], O_PS[:, :, V_IN + os_:V_IN + w], spread[:], ALU.add) \
                        .then_inc(msg_ready, 1)

                directions(Group(0, 0))
                same_rows(Group(0, 0))

                def step(g):
                    products(g)
                    if not g.is_first:
                        messages(g.prev())
                    if not g.is_last:
                        directions(g.next())
                        same_rows(g.next())
                walk(dve, step)
                messages(Group(GROUPS // 2, 0))

            edges(0)
            next_phase(dve, 2)

            def layer_norm(layer, g, base):
                b, n = g.parity, g.done(layer)
                for j in range(TILES):
                    last = dve.bn_stats(stats[:, j, :], y[:, j, :])
                last.then_inc(node_chain, 1)
                dve.wait_ge(node_chain, base + 1)
                hold(dve)
                for j in range(TILES):
                    last = dve.bn_aggr(mv[:, j, :], stats[:, j, :])
                last.then_inc(var_ready, 1)
                dve.wait_ge(std_ready, n)
                dve.reciprocal(std[:], std[:]).then_inc(node_chain, 1)
                dve.wait_ge(node_chain, base + 2)
                if layer or g.reuses:
                    dve.wait_ge(x1_out[b], 16 * (g.uses(layer) - 1))
                for j in range(TILES):
                    last = dve.tensor_scalar(x1[:, b, j, :], y[:, j, :], mv[:, j, 0:1], std[:, j:j + 1],
                                             ALU.subtract, ALU.mult)
                last.then_inc(x1_ready, 1)

            CHAIN0 = 7

            def nodes0(g):
                b, n = g.parity, g.done(0)
                base = CHAIN0 * (n - 1)

                def link(ins, k):
                    ins.then_inc(node_chain, 1)
                    dve.wait_ge(node_chain, base + k)
                dve.wait_ge(acc_in[b], 16 * TABLES * g.uses())
                dve.tensor_tensor(y[:].rearrange("p j f -> p (j f)"), accs[:, b, 0, 0:TILES * F_IN],
                                  accs[:, b, 1, 0:TILES * F_IN], ALU.add).then_inc(y_ready, 1)
                dve.wait_ge(sq_ready, n)
                dve.tensor_reduce(ms[:, 0, :], sq[:, :, 0:S_IN], AX_X, ALU.add)
                dve.tensor_reduce(ms[:, 1, :], sq[:, :, S_IN:F_IN], AX_X, ALU.add).then_inc(ms_ready, 1)
                dve.wait_ge(rms_ready, n)
                link(dve.reciprocal(rms[:], rms[:]), 1)
                for k, (a, c) in enumerate(((0, S_IN), (S_IN, F_IN))):
                    link(dve.tensor_tensor(y[:, :, a:c], y[:, :, a:c],
                                           rms[:, k, :].unsqueeze(2).broadcast_to([P, TILES, c - a]), ALU.mult), 2 + k)
                link(dve.tensor_tensor(y[:], y[:], gain[:].unsqueeze(1).broadcast_to([P, TILES, F_IN]), ALU.mult), 4)
                dve.wait_ge(x_in[b], 16 * g.uses())
                link(dve.tensor_tensor(y[:], y[:], xin[:, b], ALU.add), 5)
                layer_norm(0, g, base + 5)
                dve.wait_ge(node_mm, g.done(1))
                dve.wait_ge(sc_evac, g.done(1))
                dve.wait_ge(h_out[b], 16 * (g.uses(1) - 1))
                a = node_a[:, bass.ds(g.index * TILES, TILES)].unsqueeze(2).broadcast_to([P, TILES, F_IN])
                dve.tensor_tensor(h_sb[:, b], node_psum4(2, ACC_W[1], ACC_W[1] + F_IN), a, ALU.mult).then_inc(h_evac, 1)
            walk(dve, nodes0)
            next_phase(dve, 3)
            edges(1)
            next_phase(dve, 4)
            CHAIN1 = 5

            def nodes1(g):
                b, n = g.parity, g.done(1)
                base = CHAIN0 * GROUPS + CHAIN1 * (n - GROUPS - 1)

                def link(ins, k):
                    ins.then_inc(node_chain, 1)
                    dve.wait_ge(node_chain, base + k)
                a = node_a[:, bass.ds(g.index * TILES, TILES)].unsqueeze(2).broadcast_to([P, TILES, ACC_W[1]])
                dve.wait_ge(acc_in[b], 16 * TABLES * g.uses(1))
                link(dve.tensor_tensor(pre[:].rearrange("p j f -> p (j f)"), accs[:, b, 0], accs[:, b, 1], ALU.add), 1)
                dve.tensor_tensor(pre[:], pre[:], a, ALU.mult).then_inc(y_ready, 1)
                dve.wait_ge(sig_ready, n - GROUPS)
                dve.tensor_tensor(y[:, :, 0:S_IN], pre[:, :, 0:S_IN], sig[:, :, 0:S_IN], ALU.mult)
                gate = sig[:, :, S_IN:OUT_S[1]].unsqueeze(2).broadcast_to([P, TILES, XYZ, V_IN])
                link(dve.tensor_tensor(y[:, :, S_IN:F_IN].rearrange("p j (c u) -> p j c u", c=XYZ),
                                       pre[:, :, OUT_S[1]:ACC_W[1]].rearrange("p j (c u) -> p j c u", c=XYZ),
                                       gate, ALU.mult), 2)
                dve.wait_ge(x_in[b], 16 * g.uses(1))
                link(dve.tensor_tensor(y[:], y[:], xin[:, b], ALU.add), 3)
                layer_norm(1, g, base + 3)
            walk(dve, nodes1)
            next_phase(dve, 5)

        @block.tensor
        def _(pe):
            pe.wait_ge(weights_ready, len(scales))

            def project(layer, base, b, last_sem):
                os_, w = OUT_S[layer], ACC_W[layer]
                ws, wv = weight(f"node_s{layer}", 0, S_IN), weight(f"node_v{layer}", 0, V3)
                for j in range(TILES):
                    s, v = xs[:, b, j * P:(j + 1) * P], xv[:, b, j * P:(j + 1) * P]
                    pe.matmul(node_psum(base, j, 0, os_), s, ws[:, 0:os_], start=True, stop=True)
                    pe.matmul(node_psum(base, j, w, w + S_IN), s, ws[:, os_:os_ + S_IN], start=True, stop=True)
                    pe.matmul(node_psum(base, j, os_, w), v, wv[:, 0:V3], start=True, stop=True)
                    last = pe.matmul(node_psum(base, j, w + S_IN, w + F_IN), v, wv[:, V3:2 * V3], start=True, stop=True)
                last.then_inc(last_sem, 1)

            def nodes_in(g):
                b = g.parity
                pe.wait_ge(xT_in[b], 32 * g.uses())
                if g.reuses:
                    pe.wait_ge(sc_evac, g.done() - 2)
                    pe.wait_ge(h_evac, g.done() - 2)
                project(0, TILES * b, b, node_mm)
            walk(pe, nodes_in)
            next_phase(pe, 1)

            def edges(layer):
                os_, w = OUT_S[layer], ACC_W[layer]
                k1 = ATTR[layer]
                h0 = HID * (1 - layer)

                def hidden1(g):
                    b, n = g.parity, g.done(layer)
                    pe.wait_ge(attr_in[b], 32 * g.uses(layer))
                    hold(pe)
                    pe.matmul(H1_PS, weight(f"fc1_{layer}", 0, k1), attr[0:k1, b, :], start=True, stop=True) \
                        .then_inc(h1_mm, 1)

                def hidden2(g):
                    pe.wait_ge(h1_act, g.done(0))
                    hold(pe)
                    pe.matmul(H2_PS, weight("fc2_0", 0, HID), hidden[0:HID, :], start=True, stop=True).then_inc(h2_mm, 1)

                def edge_weights(g):
                    n = g.done(layer)
                    pe.wait_ge(h1_act if layer else h2_act, n)
                    for j in range(TILES):
                        last = pe.matmul(W_PS[:, j, 0:W_ALL], hidden[h0:h0 + HID, j * P:(j + 1) * P],
                                         weight(f"edge_w{layer}", h0, h0 + HID), start=True, stop=True)
                    last.then_inc(w_mm, 1)

                def turn(g, c):
                    n = g.done(layer)
                    c0, c1 = CHUNKS[c]
                    if c == 2:
                        pe.wait_ge(prod_ready, n)
                        pe.wait_ge(prodT_ready, 3 * (n - 1) + 1)
                    else:
                        pe.wait_ge(prod_part, 2 * (n - 1) + c + 1)
                    for j in range(TILES):
                        last = pe.transpose(T_PS[c % 2][0:c1 - c0, j * P:(j + 1) * P], prod[:, j, c0:c1], ident[:])
                    last.then_inc(prod_tr, 1)

                def project_messages(g):
                    n = g.done(layer)
                    pe.wait_ge(prodT_ready, 3 * n)
                    if not g.is_first:
                        pe.wait_ge(msg_ready, n - 1)
                        pe.wait_ge(s_ready, n - 1)
                    for j in range(TILES):
                        def pT(c, n_rows):
                            return prodT[0:n_rows, c, j * P:(j + 1) * P]
                        pe.matmul(O_PS[:, j, 0:V_IN + os_], pT(0, P), weight(f"outA{layer}", 0, P),
                                  start=True, stop=False, skip_group_check=True)
                        pe.matmul(O_PS[:, j, V_IN:V_IN + w], pT(1, P), weight(f"outB{layer}", 0, P),
                                  start=False, stop=False, skip_group_check=True)
                        last = pe.matmul(O_PS[:, j, V_IN + os_:V_IN + w], pT(2, V3), weight(f"outC{layer}", 0, V3),
                                         start=False, stop=True, skip_group_check=True)
                    last.then_inc(out_mm, 1)

                def merge(g):
                    b, n = g.parity, g.done(layer)
                    pe.wait_ge(same_ready, n)
                    pe.wait_ge(msg_ready, n)
                    pe.wait_ge(s_ready, n)
                    for q in range(2):
                        if q or not g.is_first:
                            pe.wait_ge(merged_half, 2 * (n - 1) + q)
                        for r in range(2):
                            j = 2 * q + r
                            last = pe.matmul(M_PS[:, r, 0:w], same[:, b, j, :], msg[:, j, 0:w], start=True, stop=True)
                        last.then_inc(merge_mm, 1)

                first = Group(0, 0)
                hidden1(first)
                if layer == 0:
                    hidden2(first)
                edge_weights(first)

                def step(g):
                    if not g.is_last:
                        hidden1(g.next())
                    for c in range(3):
                        turn(g, c)
                    if not g.is_last and layer == 0:
                        hidden2(g.next())
                    if not g.is_first:
                        merge(g.prev())
                    if not g.is_last:
                        edge_weights(g.next())
                    project_messages(g)
                walk(pe, step)
                merge(Group(GROUPS // 2, 0))

            edges(0)
            next_phase(pe, 2)

            def nodes_turn(g):
                b, n = g.parity, g.done(0)
                pe.wait_ge(x1_ready, n)
                hold(pe)
                for j in range(TILES):
                    pe.transpose(psum[0:S_IN, j * P:(j + 1) * P], x1[:, b, j, 0:S_IN], ident[:])
                    last = pe.transpose(psum[0:V3, BANK + j * P:BANK + (j + 1) * P], x1[:, b, j, S_IN:F_IN], ident[:])
                last.then_inc(x1_tr, 1)
                pe.wait_ge(x1T_ready, n)
                if not g.is_first:
                    pe.wait_ge(sc_evac, g.done(1) - 1)
                    pe.wait_ge(h_evac, g.done(1) - 1)
                project(1, 2, 0, node_mm)
            walk(pe, nodes_turn)
            next_phase(pe, 3)
            edges(1)
            next_phase(pe, 4)
            next_phase(pe, 5)


INS = ("x", "xT", "src_cols", "dst_cols", "src_rows", "dst_rows", "sh", "node_a", "attrT0", "attrT1", "gain",
       "sc_s0", "sc_v0", "lin_s0", "lin_v0", "fc1_0", "fc2_0", "fc_w0", "out_s0", "out_v0",
       "sc_s1", "sc_v1", "lin_s1", "lin_v1", "fc1_1", "fc_w1", "out_s1", "out_v1")


def kernel(x, src, dst, edge_attr_4, edge_attr_64, edge_attr_8, node_vec1, L0_gnn_W1_0, L0_gnn_W1_1, L0_gnn_Wfc1,
           L0_gnn_Wfc2, L0_gnn_Wfc3, L0_gnn_W2_0, L0_gnn_W2_1, L0_gnn_Wsc0, L0_gnn_Wsc1, L0_gnn_g0, L0_gnn_g1,
           L1_gnn_lin1_ws, L1_gnn_lin1_wv, L1_gnn_fc_w1, L1_gnn_fc_w2, L1_gnn_sc_ws, L1_gnn_sc_wv, L1_gnn_lin2_ws,
           L1_gnn_lin2_wv):
    import numpy as np
    import concourse.bacc as bacc
    from concourse.bass_utils import run_bass_kernel_spmd

    extra = N_PAD - N_NODES

    def padded(a, fill=0):
        return np.pad(np.asarray(a), ((0, extra),) + ((0, 0),) * (a.ndim - 1), constant_values=fill)

    def by_component(a):
        v = a[:, S_IN:].reshape(-1, V_IN, XYZ).transpose(0, 2, 1).reshape(-1, V3)
        return np.concatenate([a[:, :S_IN], v], 1)

    def columns(a):
        return a.reshape((COLS, P) + a.shape[1:]).swapaxes(0, 1).reshape(P, -1)

    xp = padded(by_component(np.asarray(x)))
    src_p, dst_p = padded(src, N_NODES), padded(dst, N_NODES)
    sh = padded(edge_attr_4)
    v = {
        "x": xp,
        "xT": xp.reshape(GROUPS, P, TILES, F_IN).transpose(0, 3, 2, 1).reshape(GROUPS, F_IN, ROWS),
        "src_cols": columns(src_p), "dst_cols": columns(dst_p),
        "src_rows": src_p.reshape(GROUPS, ROWS), "dst_rows": dst_p.reshape(GROUPS, ROWS),
        "sh": columns(np.concatenate([sh, sh[:, 1:2]], 1)),
        "node_a": padded(node_vec1).reshape(GROUPS, P, TILES).transpose(1, 0, 2).reshape(P, COLS),
        "attrT0": padded(edge_attr_8).reshape(GROUPS, ROWS, ATTR[0]).transpose(0, 2, 1),
        "attrT1": padded(edge_attr_64).reshape(GROUPS, ROWS, ATTR[1]).transpose(0, 2, 1),
        "gain": np.concatenate([np.asarray(L0_gnn_g0)] + [np.asarray(L0_gnn_g1)] * XYZ),
        "sc_s0": L0_gnn_Wsc0, "sc_v0": L0_gnn_Wsc1, "lin_s0": L0_gnn_W1_0, "lin_v0": L0_gnn_W1_1,
        "fc1_0": L0_gnn_Wfc1, "fc2_0": L0_gnn_Wfc2, "fc_w0": L0_gnn_Wfc3, "out_s0": L0_gnn_W2_0,
        "out_v0": L0_gnn_W2_1,
        "sc_s1": L1_gnn_sc_ws, "sc_v1": L1_gnn_sc_wv, "lin_s1": L1_gnn_lin1_ws, "lin_v1": L1_gnn_lin1_wv,
        "fc1_1": L1_gnn_fc_w1, "fc_w1": L1_gnn_fc_w2, "out_s1": L1_gnn_lin2_ws, "out_v1": L1_gnn_lin2_wv,
    }
    nc = bacc.Bacc("TRN2", target_bir_lowering=False, num_devices=1)
    arrays, aps = {}, {}
    for name in INS:
        a = np.ascontiguousarray(v[name])
        arrays["in_" + name] = a
        aps[name] = nc.dram_tensor("in_" + name, a.shape, mybir.dt.from_np(a.dtype), kind="ExternalInput").ap()
    out = nc.dram_tensor("out_nodes", (N_PAD, F_IN), F32, kind="ExternalOutput").ap()
    build(nc, aps, out)
    got = run_bass_kernel_spmd(nc, [arrays], core_ids=[0]).results[0]["out_nodes"][:N_NODES]
    vectors = got[:, S_IN:].reshape(-1, XYZ, V_IN).transpose(0, 2, 1).reshape(-1, V3)
    return np.concatenate([got[:, :S_IN], vectors], 1)
```

```python
from contextlib import ExitStack

import concourse.bass as bass
import concourse.mybir as mybir
from concourse.alu_op_type import AluOpType as ALU

ACT = mybir.ActivationFunctionType
F32 = mybir.dt.float32
I32 = mybir.dt.int32
AX_X = mybir.AxisListType.X

P = 128
TILES = 4
ROWS = P * TILES
N_NODES = 25000
GROUPS = -(-N_NODES // ROWS)
N_PAD = GROUPS * ROWS
COLS = GROUPS * TILES
TABLES = 2
S_IN, V_IN, XYZ = 64, 32, 3
V3 = V_IN * XYZ
F_IN = S_IN + V3
HID = 64
W_ALL = 2 * S_IN + 3 * V_IN
OUT_S = (64, 96)
ATTR = (8, 64)
SLOT = 256
BANK = 512
EPS = 1e-5
NEIGHBOURS = 16.0
HIDDEN_SCALE = (ATTR[0] ** -0.5, ATTR[1] ** -0.5)

def _columns(widths):
    at, out = 0, {}
    for name, n in widths:
        out[name] = (at, at + n)
        at += n
    return out, at


WEIGHT_COLS, WEIGHT_WIDTH = _columns([
    ("node_a0", 128 + 64 + 64), ("node_b0", 2 * V_IN), ("node_a1", 128 + 96 + 64), ("node_b1", 2 * V_IN),
    ("fc1_0", HID), ("fc2_0", HID), ("edge_w0", W_ALL), ("fc1_1", HID), ("edge_w1", W_ALL),
    ("outA0", V_IN + 64), ("outB0", 64 + V3), ("outC0", V3),
    ("outA1", V_IN + 96), ("outB1", 96 + V3), ("outC1", V3)])


class Group:

    def __init__(self, half, parity):
        self.half, self.parity = half, parity
        self.index = 2 * half + parity
        self.static = isinstance(half, int)
        self.reuses = not (self.static and half <= 0)
        self.is_first = self.static and self.index == 0
        self.is_last = self.static and self.index == GROUPS - 1

    def at(self, offset):
        halves, parity = divmod(self.parity + offset, 2)
        g = Group(self.half + halves, parity)
        return None if g.static and not 0 <= g.index < GROUPS else g

    def done(self, layer=0):
        return layer * GROUPS + self.index + 1

    def uses(self, layer=0):
        return layer * ((GROUPS + 1 - self.parity) // 2) + self.half + 1


def walk(eng, *stages):
    def step(g):
        for offset, stage in stages:
            if g.at(offset) is not None:
                stage(g.at(offset))
    for first in range(-max(offset for offset, _ in stages), 4):
        step(Group(first // 2, first % 2))
    with eng.Fori(2, GROUPS // 2) as i:
        step(Group(i, 0))
        step(Group(i, 1))
    for last in range(GROUPS - 1, GROUPS - min(0, min(offset for offset, _ in stages))):
        step(Group(last // 2, last % 2))


def build(nc, t, out):
    ctx = ExitStack()
    with ctx:
        def sb(name, shape, dt=F32):
            return ctx.enter_context(nc.sbuf_tensor(name, shape, dt))

        def ps(name, shape):
            return ctx.enter_context(nc.psum_tensor(name, shape, F32))

        def sem(name):
            return ctx.enter_context(nc.semaphore(name))

        def sem2(name):
            return [sem(f"{name}{b}") for b in range(2)]

        def dram(name, shape):
            return nc.dram_tensor(name, shape, F32).ap()

        h_tab = [dram("h_tab0", (N_PAD, F_IN)), dram("h_tab1", (N_PAD, F_IN))]
        ACC_W = [OUT_S[0] + V3, OUT_S[1] + V3]
        acc_tab = [[dram(f"acc_tab{l}{k}", (N_PAD + P, ACC_W[l])) for k in range(TABLES)] for l in range(2)]
        x1_tab = dram("x1_tab", (N_PAD, F_IN))

        def rows(tab, g):
            r0 = g.index * ROWS
            return tab[bass.ds(r0, ROWS), :].rearrange("(p j) f -> p (j f)", j=TILES)

        W = sb("W", [P, WEIGHT_WIDTH])
        ident = sb("ident", [P, P])
        before = sb("before", [P, P])
        gain = sb("gain", [P, F_IN])
        eps = sb("eps", [P, 1])
        dump_row = sb("dump_row", [P, 1])
        zeros = sb("zeros", [P, TILES * ACC_W[1]])
        idx_i = [sb("src_i", [P, COLS], I32), sb("dst_i", [P, COLS], I32)]
        idx_f = [sb("src_f", [P, COLS]), sb("dst_f", [P, COLS])]
        repeats = sb("repeats", [P, 2, TILES])
        to_dump = sb("to_dump", [P, 2, COLS])
        sh = sb("sh", [P, COLS, 5])
        node_a = sb("node_a", [P, COLS])
        read_now = sb("read_now", [P, 2, TILES], I32)
        add_now = sb("add_now", [P, 2, TILES], I32)
        dump_part = sb("dump_part", [P, TILES])
        read_now_ready, add_now_ready, dump_part_ready = sem("read_now_ready"), sem("add_now_ready"), sem("dump_part_ready")
        zero1_out = sem("zero1_out")

        def weight(name, p0, p1):
            c0, c1 = WEIGHT_COLS[name]
            return W[p0:p1, c0:c1]

        idx_row = sb("idx_row", [P, 2, ROWS], I32)
        xa = sb("xa", [P, 2, ROWS])
        xz = sb("xz", [V_IN, 2, ROWS])
        sc_sb = sb("sc_sb", [P, 2, TILES, ACC_W[1]])
        h_sb = sb("h_sb", [P, 2, TILES, F_IN])
        junk = sb("junk", [P, TILES, P])

        hg = sb("hg", [P, 2, TILES, F_IN])
        attr = sb("attr", [HID, 2, ROWS])
        hidden = sb("hidden", [P, ROWS])
        U = sb("U", [P, 2, TILES, 288])
        crossed = sb("crossed", [P, TILES, V3])
        prod = sb("prod", [P, TILES, 352])
        prodT = sb("prodT", [P, 3, ROWS])
        same = sb("same", [P, 2, TILES, P])
        pw_sb = sb("pw_sb", [P, TILES, V_IN])
        spread = sb("spread", [P, TILES, V3])
        msg = sb("msg", [P, TILES, ACC_W[1]])
        merged = sb("merged", [P, 2, TILES, ACC_W[1]])

        accs = sb("accs", [P, 2, TABLES, TILES * ACC_W[1]])
        xin = sb("xin", [P, 2, TILES, F_IN])
        y = sb("y", [P, 2, TILES, F_IN])
        total = sb("total", [P, 2, TILES, ACC_W[1]])
        sq = sb("sq", [P, TILES, F_IN])
        ms = sb("ms", [P, 2, 2, TILES])
        rms = sb("rms", [P, 2, 2, TILES])
        stats = sb("stats", [P, TILES, 6])
        mv = sb("mv", [P, 2, TILES, 2])
        std = sb("std", [P, 2, TILES])
        x1 = sb("x1", [P, 2, TILES, F_IN])

        psum = ps("psum", [P, 8 * BANK])

        consts_ready, weights_in, weights_zero, weights_ready = (
            sem("consts_ready"), sem("weights_in"), sem("weights_zero"), sem("weights_ready"))
        tables_in = sem("tables_in")
        idx_float, phase_end = sem("idx_float"), sem("phase_end")
        xT_in, idx_row_in = sem2("xT_in"), sem2("idx_row_in")
        node_mm, sc_evac, h_evac = sem("node_mm"), sem("sc_evac"), sem("h_evac")
        sc_out, h_out, zero_out = sem2("sc_out"), sem2("h_out"), sem("zero_out")
        counted, to_dump_ready = sem("counted"), sem("to_dump_ready")

        attr_in, hg_in = sem2("attr_in"), sem2("hg_in")
        h1_mm, h1_act, h2_mm, h2_act, w_mm = (sem("h1_mm"), sem("h1_act"), sem("h2_mm"), sem("h2_act"), sem("w_mm"))
        u_dot, u_ready = sem("u_dot"), sem("u_ready")
        prod_ready, prod_tr, prodT_ready = sem("prod_ready"), sem("prod_tr"), sem("prodT_ready")
        out_mm, pw_ready, s_ready, spread_ready, msg_ready = (
            sem("out_mm"), sem("pw_ready"), sem("s_ready"), sem("spread_ready"), sem("msg_ready"))
        same_ready, merge_mm = sem("same_ready"), sem("merge_mm")
        added = [sem(f"added{k}") for k in range(TABLES)]

        acc_in, x_in, x1_out = sem2("acc_in"), sem2("x_in"), sem2("x1_out")
        prod_part, merged_half = sem("prod_part"), sem("merged_half")
        sig = sb("sig", [P, TILES, OUT_S[1]])
        sq_ready, rms_ready, std_ready = sem("sq_ready"), sem("rms_ready"), sem("std_ready")
        ms_ready, var_ready, x1_ready = sem("ms_ready"), sem("var_ready"), sem("x1_ready")
        x1_tr, x1T_ready = sem("x1_tr"), sem("x1T_ready")
        total_sum, total_ready, sig_ready, gated = sem("total_sum"), sem("total_ready"), sem("sig_ready"), sem("gated")
        scaled, y_sum, bn_done, inverse_rms, inverse_std = (
            sem("scaled"), sem("y_sum"), sem("bn_done"), sem("inverse_rms"), sem("inverse_std"))

        ENGINES = 5

        def next_phase(eng, k):
            eng.drain().then_inc(phase_end, 1)
            eng.wait_ge(phase_end, ENGINES * k)

        waits_held = sem("waits_held")

        def hold(eng):
            eng.sem_inc(waits_held, 1)

        def blocks(name, p0, c0, src):
            first = WEIGHT_COLS[name][0]
            return [(W[p0 + V_IN * c:p0 + V_IN * (c + 1), first + c0 + V_IN * c:first + c0 + V_IN * (c + 1)], src)
                    for c in range(XYZ)]

        def part(name, p0, p1, c0, c1, src):
            first = WEIGHT_COLS[name][0]
            return [(W[p0:p1, first + c0:first + c1], src)]

        weight_dmas = []
        for l in range(2):
            sc, scv, lin, linv = t[f"sc_s{l}"], t[f"sc_v{l}"], t[f"lin_s{l}"], t[f"lin_v{l}"]
            os_ = OUT_S[l]
            weight_dmas += part(f"node_a{l}", 0, S_IN, 0, S_IN, lin)
            weight_dmas += part(f"node_a{l}", 0, S_IN, P, P + os_, sc)
            for c in range(2):
                p0 = S_IN + V_IN * c
                weight_dmas += part(f"node_a{l}", p0, p0 + V_IN, p0, p0 + V_IN, linv)
                weight_dmas += part(f"node_a{l}", p0, p0 + V_IN, P + os_ + V_IN * c, P + os_ + V_IN * (c + 1), scv)
            weight_dmas += part(f"node_b{l}", 0, V_IN, 0, V_IN, scv) + part(f"node_b{l}", 0, V_IN, V_IN, 2 * V_IN, linv)
            fc, q0 = t[f"fc_w{l}"], HID * (1 - l)
            for c0, c1, f0 in ((0, 64, 64), (64, 128, 0), (128, W_ALL, 128)):
                weight_dmas += part(f"edge_w{l}", q0, q0 + HID, c0, c1, fc[:, f0:f0 + c1 - c0])
            o_s, o_v = t[f"out_s{l}"], t[f"out_v{l}"]
            weight_dmas += part(f"outA{l}", 0, 64, 0, V_IN, o_v[0:64, :])
            weight_dmas += part(f"outA{l}", 64, 128, V_IN, V_IN + os_, o_s[0:64, :])
            weight_dmas += part(f"outB{l}", V3, P, 0, os_, o_s[64:96, :])
            weight_dmas += blocks(f"outB{l}", 0, os_, o_v[64:96, :]) + blocks(f"outC{l}", 0, 0, o_v[96:128, :])
        weight_dmas += part("fc1_0", 0, ATTR[0], 0, HID, t["fc1_0"])
        weight_dmas += part("fc2_0", 0, HID, 0, HID, t["fc2_0"])
        weight_dmas += part("fc1_1", 0, HID, 0, HID, t["fc1_1"])

        scales = []
        for l in range(2):
            def cols(name, a, b):
                c = WEIGHT_COLS[name][0]
                return (c + a, c + b)
            os_ = OUT_S[l]
            f_s = (96 * NEIGHBOURS) ** -0.5
            f_v = (128 * NEIGHBOURS) ** -0.5
            scales += [(cols(f"node_a{l}", 0, S_IN), S_IN ** -0.5), (cols(f"node_a{l}", S_IN, P), V_IN ** -0.5),
                       (cols(f"node_a{l}", P, P + os_), S_IN ** -0.5),
                       (cols(f"node_a{l}", P + os_, P + os_ + 2 * V_IN), V_IN ** -0.5),
                       (cols(f"node_b{l}", 0, 2 * V_IN), V_IN ** -0.5),
                       (cols(f"edge_w{l}", 0, 160), HID ** -0.5),
                       (cols(f"edge_w{l}", 160, 192), (HID * 3) ** -0.5),
                       (cols(f"edge_w{l}", 192, 224), (HID * 2) ** -0.5),
                       (cols(f"outA{l}", 0, V_IN), f_v), (cols(f"outA{l}", V_IN, V_IN + os_), f_s),
                       (cols(f"outB{l}", 0, os_), f_s), (cols(f"outB{l}", os_, os_ + V3), f_v),
                       (cols(f"outC{l}", 0, V3), f_v)]

        def node_psum(base, j, a, b):
            return psum[:, (base + j) * BANK + a:(base + j) * BANK + b]

        def node_psum4(base, a, b):
            return psum[:, base * BANK:(base + TILES) * BANK].rearrange("p (j c) -> p j c", j=TILES)[:, :, a:b]

        H1_PS = psum[0:HID, 0:BANK]
        H2_PS = psum[HID:P, 0:BANK]
        W_PS = psum[:, BANK:3 * BANK].rearrange("p (j c) -> p j c", c=SLOT)
        T_PS = [psum[:, 3 * BANK:4 * BANK], psum[:, 4 * BANK:5 * BANK]]
        O_PS = psum[:, 5 * BANK:7 * BANK].rearrange("p (j c) -> p j c", c=SLOT)
        M_PS = psum[:, 7 * BANK:8 * BANK].rearrange("p (j c) -> p j c", c=SLOT)
        CHUNKS = ((0, 128), (128, 256), (256, 352))

        block = ctx.enter_context(nc.Block())

        @block.sync
        def _(sp):
            for k in range(2):
                sp.dma_start(idx_i[k][:], t[("src", "dst")[k] + "_cols"][:]).then_inc(tables_in, 16)
            sp.dma_start(sh[:], t["sh"].rearrange("p (c k) -> p c k", k=5)).then_inc(tables_in, 16)
            sp.dma_start(node_a[:], t["node_a"]).then_inc(tables_in, 16)
            sp.dma_start(gain[:], t["gain"].partition_broadcast(P)).then_inc(tables_in, 16)
            sp.wait_ge(weights_zero, 1)
            for dst, src in weight_dmas:
                sp.dma_start(dst, src).then_inc(weights_in, 16)

            def load_nodes(g):
                b = g.parity
                if g.reuses:
                    sp.wait_ge(node_mm, g.done() - 2)
                sp.dma_start(xa[:, b, :], t["xT"][g.index, 0:P, :]).then_inc(xT_in[b], 16)
                sp.dma_start(xz[:, b, :], t["xT"][g.index, P:F_IN, :]).then_inc(xT_in[b], 16)
            walk(sp, (0, load_nodes))
            next_phase(sp, 1)

            def load_edges(layer):
                k_add = ("src", "dst")[layer] + "_rows"

                def step(g):
                    b = g.parity
                    if g.reuses:
                        sp.wait_ge(h1_mm, g.done(layer) - 2)
                        sp.wait_ge(same_ready, g.done(layer) - 2)
                    sp.dma_start(attr[0:ATTR[layer], b, :], t[f"attrT{layer}"][g.index]).then_inc(attr_in[b], 16)
                    sp.dma_start(idx_row[:, b, :], t[k_add][g.index, :].partition_broadcast(P)).then_inc(attr_in[b], 16)
                    if layer == 0:
                        for k in range(1, TABLES):
                            sp.dma_start(rows(acc_tab[1][k], g), zeros[:, 0:TILES * ACC_W[1]]).then_inc(zero1_out, 16)
                walk(sp, (0, step))

            def load_sums(layer, x_src):
                w = ACC_W[layer]

                def step(g):
                    b = g.parity
                    if g.reuses:
                        sp.wait_ge(total_sum, g.done(layer) - 2)
                    for k in range(TABLES):
                        sp.dma_start(accs[:, b, k, 0:TILES * w], rows(acc_tab[layer][k], g)).then_inc(acc_in[b], 16)
                    if g.reuses:
                        sp.wait_ge(y_sum, g.done(layer) - 2)
                    sp.dma_start(xin[:, b, :, :].rearrange("p j f -> p (j f)"), rows(x_src, g)).then_inc(x_in[b], 16)
                walk(sp, (0, step))

            load_edges(0)
            sp.wait_ge(zero1_out, 16 * GROUPS * (TABLES - 1))
            next_phase(sp, 2)
            load_sums(0, t["x"])
            next_phase(sp, 3)
            load_edges(1)
            next_phase(sp, 4)
            load_sums(1, x1_tab)
            next_phase(sp, 5)

        @block.gpsimd
        def _(pool):
            pool.memset(W[:], 0.0).then_inc(weights_zero, 1)
            pool.memset(ident[:], 0.0).then_inc(consts_ready, 1)
            pool.memset(before[:], 1.0).then_inc(consts_ready, 1)
            pool.memset(eps[:], EPS).then_inc(consts_ready, 1)
            pool.memset(zeros[:], 0.0).then_inc(consts_ready, 1)
            pool.iota(dump_row[:], pattern=[[0, 1]], base=N_PAD, channel_multiplier=1,
                      allow_small_or_imprecise_dtypes=True).then_inc(consts_ready, 1)
            pool.wait_ge(consts_ready, 5)
            pool.affine_select(out=ident[:], in_=ident[:], compare_op=ALU.not_equal, fill=1.0, base=0,
                               pattern=[[-1, P]], channel_multiplier=1).then_inc(consts_ready, 1)
            pool.affine_select(out=before[:], in_=before[:], compare_op=ALU.is_gt, fill=0.0, base=0,
                               pattern=[[-1, P]], channel_multiplier=1).then_inc(consts_ready, 1)

            next_phase(pool, 1)

            def edges(layer):
                gather_by = idx_i[1 - layer]
                w = ACC_W[layer]

                def indices(g):
                    b = g.parity
                    if g.reuses:
                        pool.wait_ge(prod_ready, g.done(layer) - 2)
                        pool.wait_ge(u_ready, g.done(layer) - 2)
                    pool.tensor_copy(read_now[:, b, :], gather_by[:, bass.ds(g.index * TILES, TILES)]) \
                        .then_inc(read_now_ready, 1)
                    pool.wait_ge(read_now_ready, g.done(layer))
                    hold(pool)

                def gather(g, tiles):
                    b = g.parity
                    for j in tiles:
                        pool.indirect_dma_start(
                            out=hg[:, b, j, :], out_offset=None, in_=h_tab[layer][:, :],
                            in_offset=bass.IndirectOffsetOnAxis(ap=read_now[:, b, j:j + 1], axis=0)) \
                            .then_inc(hg_in[b], 16)

                def scatter(g, q):
                    b = g.parity
                    pool.wait_ge(add_now_ready, g.done(layer))
                    pool.wait_ge(merged_half, 2 * (g.done(layer) - 1) + q + 1)
                    hold(pool)
                    for j in range(2 * q, 2 * q + 2):
                        k = j % TABLES
                        before_this = layer * COLS // TABLES + g.index * (TILES // TABLES) + j // TABLES
                        if not g.static or before_this:
                            pool.wait_ge(added[k], 16 * before_this)
                            hold(pool)
                        pool.indirect_dma_start(
                            out=acc_tab[layer][k][:, :],
                            out_offset=bass.IndirectOffsetOnAxis(ap=add_now[:, b, j:j + 1], axis=0),
                            in_=merged[:, b, j, 0:w], in_offset=None, compute_op=ALU.add).then_inc(added[k], 16)

                walk(pool, (1, indices), (1, lambda g: gather(g, (0, 1))), (-2, lambda g: scatter(g, 0)),
                     (1, lambda g: gather(g, (2, 3))), (-2, lambda g: scatter(g, 1)))
                for k in range(TABLES):
                    pool.wait_ge(added[k], 16 * (layer + 1) * COLS // TABLES)

            def totals(layer):
                w = ACC_W[layer]

                def flat(g):
                    return total[:, g.parity].rearrange("p j f -> p (j f)")[:, 0:TILES * w]

                def add_tables(g):
                    b, n = g.parity, g.done(layer)
                    pool.wait_ge(acc_in[b], 16 * TABLES * g.uses(layer))
                    if g.reuses:
                        if layer == 0:
                            pool.wait_ge(sq_ready, n - 2)
                            pool.wait_ge(total_ready, n - 2)
                        else:
                            pool.wait_ge(gated, g.done() - 2)
                    pool.tensor_tensor(flat(g), accs[:, b, 0, 0:TILES * w], accs[:, b, 1, 0:TILES * w], ALU.add) \
                        .then_inc(total_sum, 1)

                def factor_in(g):
                    b, n = g.parity, g.done(layer)
                    pool.wait_ge(total_sum, n)
                    if layer == 0 and g.reuses:
                        pool.wait_ge(x1_ready, n - 2)
                    tot = flat(g).rearrange("p (j f) -> p j f", j=TILES)
                    if layer == 0:
                        factor = gain[:].unsqueeze(1).broadcast_to([P, TILES, w])
                    else:
                        factor = node_a[:, bass.ds(g.index * TILES, TILES)].unsqueeze(2).broadcast_to([P, TILES, w])
                    pool.tensor_tensor(y[:, b] if layer == 0 else tot, tot, factor, ALU.mult).then_inc(total_ready, 1)
                walk(pool, (1 - layer, add_tables), (0, factor_in))

            edges(0)
            next_phase(pool, 2)
            totals(0)
            next_phase(pool, 3)
            edges(1)
            next_phase(pool, 4)
            totals(1)
            next_phase(pool, 5)

        @block.scalar
        def _(act):
            act.wait_ge(consts_ready, 7)
            for l in range(2):
                for k in range(TABLES):
                    act.dma_start(acc_tab[l][k][N_PAD:N_PAD + P, :], zeros[:, 0:ACC_W[l]]).then_inc(zero_out, 16)

            def project_out(layer, g, base):
                b, w = g.parity, ACC_W[layer]
                act.wait_ge(node_mm, g.done(layer))
                if g.reuses:
                    act.wait_ge(sc_out[b], 16 * (g.uses(layer) - 1))
                sc_buf = sc_sb[:, b].rearrange("p j f -> p (j f)")[:, 0:TILES * w]
                act.activation(sc_buf.rearrange("p (j f) -> p j f", j=TILES), node_psum4(base, P, P + w),
                               ACT.Copy).then_inc(sc_evac, 1)
                act.wait_ge(sc_evac, g.done(layer))
                act.dma_start(rows(acc_tab[layer][0], g), sc_buf).then_inc(sc_out[b], 16)
                if layer == 0:
                    for k in range(1, TABLES):
                        act.dma_start(rows(acc_tab[0][k], g), zeros[:, 0:TILES * w]).then_inc(zero_out, 16)

            def features_out(layer, g):
                b = g.parity
                act.wait_ge(h_evac, g.done(layer))
                act.dma_start(rows(h_tab[layer], g), h_sb[:, b].rearrange("p j f -> p (j f)")).then_inc(h_out[b], 16)

            def stores_landed(layer):
                for b in range(2):
                    last = (layer + 1) * ((GROUPS + 1 - b) // 2)
                    act.wait_ge(sc_out[b], 16 * last)
                    act.wait_ge(h_out[b], 16 * last)
                act.wait_ge(zero_out, 16 * (2 * TABLES + GROUPS * (TABLES - 1)))

            walk(act, (0, lambda g: project_out(0, g, TILES * g.parity)), (-1, lambda g: features_out(0, g)))
            stores_landed(0)
            next_phase(act, 1)

            def edges(layer):
                os_, w = OUT_S[layer], ACC_W[layer]

                def first_silu(g):
                    n = g.done(layer)
                    act.wait_ge(h1_mm, n)
                    act.activation(hidden[0:HID, :], H1_PS, ACT.Silu, scale=HIDDEN_SCALE[layer]).then_inc(h1_act, 1)

                def second_silu(g):
                    act.wait_ge(h2_mm, g.done(0))
                    act.activation(hidden[HID:P, :], H2_PS, ACT.Silu, scale=HID ** -0.5).then_inc(h2_act, 1)

                def turned_out(g, c):
                    n3 = 3 * (g.done(layer) - 1) + c + 1
                    n_rows = CHUNKS[c][1] - CHUNKS[c][0]
                    act.wait_ge(prod_tr, n3)
                    act.activation(prodT[0:n_rows, c, :], T_PS[c % 2][0:n_rows, :], ACT.Copy).then_inc(prodT_ready, 1)

                def merged_out(g):
                    b = g.parity
                    if g.reuses:
                        for k in range(TABLES):
                            base = layer * COLS // TABLES
                            act.wait_ge(added[k], 16 * (base + (g.index - 1) * (TILES // TABLES)))
                    for q in range(2):
                        act.wait_ge(merge_mm, 2 * (g.done(layer) - 1) + q + 1)
                        act.activation(merged[:, b, 2 * q:2 * q + 2, 0:w], M_PS[:, :, 0:w], ACT.Copy) \
                            .then_inc(merged_half, 1)

                def message_out(g):
                    n = g.done(layer)
                    act.wait_ge(out_mm, n)
                    if not g.is_first:
                        act.wait_ge(spread_ready, n - 1)
                    act.activation(pw_sb[:], O_PS[:, :, 0:V_IN], ACT.Copy).then_inc(pw_ready, 1)
                    if not g.is_first:
                        act.wait_ge(merge_mm, 2 * (n - 1))
                    act.activation(msg[:, :, 0:os_], O_PS[:, :, V_IN:V_IN + os_], ACT.Copy).then_inc(s_ready, 1)

                walk(act, (1, first_silu), (0, lambda g: turned_out(g, 0)), (0, lambda g: turned_out(g, 1)),
                     (0, lambda g: turned_out(g, 2)), *[(1, second_silu)] * (1 - layer), (-1, merged_out),
                     (0, message_out))

            edges(0)
            next_phase(act, 2)

            def squares(g):
                act.wait_ge(total_sum, g.done())
                if not g.is_first:
                    act.wait_ge(ms_ready, g.done() - 1)
                act.activation(sq[:].rearrange("p j f -> p (j f)"),
                               total[:, g.parity].rearrange("p j f -> p (j f)")[:, 0:TILES * F_IN],
                               ACT.Square).then_inc(sq_ready, 1)

            def root_mean_squares(g):
                b = g.parity
                act.wait_ge(ms_ready, g.done())
                for k, n_channels in enumerate((S_IN, V_IN)):
                    act.activation(rms[:, b, k, :], ms[:, b, k, :], ACT.Sqrt, bias=eps[:, 0:1],
                                   scale=1.0 / n_channels).then_inc(rms_ready, 1)

            def deviation(layer, g):
                act.wait_ge(var_ready, g.done(layer))
                act.activation(std[:, g.parity], mv[:, g.parity, :, 1], ACT.Sqrt, bias=eps[:, 0:1], scale=1.0).then_inc(std_ready, 1)

            def store_nodes(layer, g):
                act.wait_ge(x1_ready, g.done(layer))
                dst = x1_tab if layer == 0 else out
                act.dma_start(rows(dst, g), x1[:, g.parity].rearrange("p j f -> p (j f)")).then_inc(x1_out[g.parity], 16)

            def turned_nodes(g):
                act.wait_ge(x1_tr, g.done())
                act.activation(xa[:, 0, :], psum[:, 0:BANK], ACT.Copy).then_inc(x1T_ready, 1)
                act.activation(xz[:, 0, :], psum[0:V_IN, BANK:2 * BANK], ACT.Copy).then_inc(x1T_ready, 1)

            walk(act, (-1, lambda g: deviation(0, g)), (-3, lambda g: project_out(1, g, 2)), (1, squares),
                 (-2, lambda g: store_nodes(0, g)), (-2, turned_nodes), (1, root_mean_squares),
                 (-3, lambda g: features_out(1, g)))
            stores_landed(1)
            for b in range(2):
                act.wait_ge(x1_out[b], 16 * ((GROUPS + 1 - b) // 2))
            next_phase(act, 3)
            edges(1)
            next_phase(act, 4)

            def gates(g):
                act.wait_ge(total_ready, g.done(1))
                if not g.is_first:
                    act.wait_ge(gated, g.done() - 1)
                act.activation(sig[:], total[:, g.parity, :, 0:OUT_S[1]], ACT.Sigmoid).then_inc(sig_ready, 1)
            walk(act, (-1, lambda g: deviation(1, g)), (1, gates), (-2, lambda g: store_nodes(1, g)))
            for b in range(2):
                act.wait_ge(x1_out[b], 16 * 2 * ((GROUPS + 1 - b) // 2))
            next_phase(act, 5)

        @block.vector
        def _(dve):
            dve.wait_ge(weights_in, 16 * len(weight_dmas))
            for (c0, c1), f in scales:
                dve.tensor_scalar(W[:, c0:c1], W[:, c0:c1], f, None, ALU.mult).then_inc(weights_ready, 1)
            dve.wait_ge(tables_in, 16 * 5)
            dve.wait_ge(consts_ready, 7)
            for k in range(2):
                dve.tensor_copy(idx_f[k][:], idx_i[k][:]).then_inc(idx_float, 1)
            dve.wait_ge(idx_float, 2)

            def node_features(g):
                b = g.parity
                dve.wait_ge(node_mm, g.done())
                if g.reuses:
                    dve.wait_ge(h_out[b], 16 * (g.uses() - 1))
                dve.wait_ge(sc_evac, g.done())
                dve.tensor_copy(h_sb[:, b, :, 0:P], node_psum4(TILES * b, 0, P))
                dve.tensor_copy(h_sb[:, b, :, P:F_IN], node_psum4(TILES * b, P + ACC_W[0], F_IN + ACC_W[0])) \
                    .then_inc(h_evac, 1)
            walk(dve, (0, node_features))
            for k in range(2):
                dve.tensor_scalar(to_dump[:, k], idx_f[k][:], -1.0, dump_row[:, 0:1], ALU.mult, ALU.add) \
                    .then_inc(to_dump_ready, 1)
            dve.wait_ge(to_dump_ready, 2)
            next_phase(dve, 1)

            def edges(layer):
                os_, w = OUT_S[layer], ACC_W[layer]

                def edge_sh(g, k, n, width):
                    v = sh[:, bass.ds(g.index * TILES, TILES), k:k + n]
                    return v.unsqueeze(3).broadcast_to([P, TILES, n, width])

                def directions(g):
                    b, n = g.parity, g.done(layer)
                    s, v = hg[:, b, :, 0:S_IN], hg[:, b, :, S_IN:F_IN].rearrange("p j (c u) -> p j c u", c=XYZ)
                    cross = U[:, b, :, 192:288].rearrange("p j (c u) -> p j c u", c=XYZ)
                    other = crossed[:].rearrange("p j (c u) -> p j c u", c=XYZ)
                    dve.wait_ge(hg_in[b], 16 * TILES * g.uses(layer))
                    dve.tensor_tensor(U[:, b, :, 0:F_IN], hg[:, b], edge_sh(g, 0, 1, F_IN)[:, :, 0, :], ALU.mult)
                    dve.tensor_tensor(cross[:, :, 0:2], v[:, :, 1:3], edge_sh(g, 3, 2, V_IN), ALU.mult)
                    dve.tensor_tensor(cross[:, :, 2:3], v[:, :, 0:1], edge_sh(g, 2, 1, V_IN), ALU.mult)
                    dve.tensor_tensor(other[:, :, 1:3], v[:, :, 0:2], edge_sh(g, 3, 2, V_IN), ALU.mult)
                    dve.tensor_tensor(other[:, :, 0:1], v[:, :, 2:3], edge_sh(g, 2, 1, V_IN), ALU.mult) \
                        .then_inc(u_dot, 1)
                    dve.wait_ge(u_dot, 4 * (n - 1) + 1)
                    dve.tensor_tensor(cross, cross, other, ALU.subtract).then_inc(u_dot, 1)
                    dve.wait_ge(u_dot, 4 * (n - 1) + 2)
                    dve.tensor_tensor(other, v, edge_sh(g, 1, 3, V_IN), ALU.mult).then_inc(u_dot, 1)
                    dve.wait_ge(u_dot, 4 * (n - 1) + 3)
                    dot = U[:, b, :, 160:192]
                    dve.tensor_tensor(dot, other[:, :, 0], other[:, :, 1], ALU.add).then_inc(u_dot, 1)
                    dve.wait_ge(u_dot, 4 * n)
                    dve.tensor_tensor(dot, dot, other[:, :, 2], ALU.add).then_inc(u_ready, 1)

                def same_rows(g):
                    b, n = g.parity, g.done(layer)
                    dve.wait_ge(attr_in[b], 32 * g.uses(layer))
                    if g.reuses:
                        dve.wait_ge(merge_mm, 2 * (n - 2))
                    own = idx_f[layer][:, bass.ds(g.index * TILES, TILES)].unsqueeze(2).broadcast_to([P, TILES, P])
                    idx_q = idx_row[:, b, :].rearrange("p (j q) -> p j q", j=TILES)
                    if layer or not g.is_first:
                        dve.wait_ge(counted, TILES * (n - 1))
                    for j in range(TILES):
                        dve.scalar_tensor_tensor(
                            out=junk[:, j, :], in0=idx_q[:, j, :],
                            scalar=idx_f[layer][:, bass.ds(g.index * TILES + j, 1)], in1=before[:], op0=ALU.is_equal,
                            op1=ALU.mult, accum_out=repeats[:, b, j:j + 1]).then_inc(counted, 1)
                    dve.tensor_tensor(same[:, b], idx_q, own, ALU.is_equal).then_inc(same_ready, 1)

                def rows_to_add(g):
                    b, n = g.parity, g.done(layer)
                    dve.wait_ge(counted, TILES * n)
                    cols = bass.ds(g.index * TILES, TILES)
                    dve.scalar_tensor_tensor(out=dump_part[:], in0=repeats[:, b, :], scalar=1.0,
                                             in1=to_dump[:, layer, cols], op0=ALU.min, op1=ALU.mult) \
                        .then_inc(dump_part_ready, 1)
                    dve.wait_ge(dump_part_ready, n)
                    if g.reuses:
                        base = layer * COLS // TABLES
                        for k in range(TABLES):
                            dve.wait_ge(added[k], 16 * (base + (g.index - 1) * (TILES // TABLES)))
                    dve.tensor_tensor(add_now[:, b, :], dump_part[:], idx_f[layer][:, cols], ALU.add) \
                        .then_inc(add_now_ready, 1)

                def products(g):
                    b, n = g.parity, g.done(layer)
                    dve.wait_ge(w_mm, n)
                    dve.wait_ge(u_ready, n)
                    dve.tensor_tensor(prod[:, :, 0:64], W_PS[:, :, 0:64], hg[:, b, :, 0:S_IN], ALU.mult)
                    dve.tensor_tensor(prod[:, :, 64:128], W_PS[:, :, 64:128], U[:, b, :, 0:64], ALU.mult) \
                        .then_inc(prod_part, 1)

                    def spread_w(c0):
                        return W_PS[:, :, c0:c0 + V_IN].unsqueeze(2).broadcast_to([P, TILES, XYZ, V_IN])

                    def xyz(ap):
                        return ap.rearrange("p j (c u) -> p j c u", c=XYZ)
                    dve.tensor_tensor(xyz(prod[:, :, 128:224]), spread_w(128), xyz(U[:, b, :, 64:160]), ALU.mult)
                    dve.tensor_tensor(prod[:, :, 224:256], W_PS[:, :, 160:192], U[:, b, :, 160:192], ALU.mult) \
                        .then_inc(prod_part, 1)
                    dve.tensor_tensor(xyz(prod[:, :, 256:352]), spread_w(192), xyz(U[:, b, :, 192:288]), ALU.mult) \
                        .then_inc(prod_ready, 1)

                def messages(g):
                    n = g.done(layer)
                    dve.wait_ge(pw_ready, n)
                    pw = pw_sb[:].unsqueeze(2).broadcast_to([P, TILES, XYZ, V_IN])
                    dve.tensor_tensor(spread[:].rearrange("p j (c u) -> p j c u", c=XYZ), pw,
                                      edge_sh(g, 1, 3, V_IN), ALU.mult).then_inc(spread_ready, 1)
                    dve.wait_ge(spread_ready, n)
                    dve.wait_ge(s_ready, n)
                    if not g.is_first:
                        dve.wait_ge(merge_mm, 2 * (n - 1))
                    dve.tensor_tensor(msg[:, :, os_:w], O_PS[:, :, V_IN + os_:V_IN + w], spread[:], ALU.add) \
                        .then_inc(msg_ready, 1)

                walk(dve, (0, products), (-1, messages), (-1, rows_to_add), (1, directions), (1, same_rows))

            edges(0)
            next_phase(dve, 2)

            def sum_squares(g):
                b = g.parity
                dve.wait_ge(sq_ready, g.done())
                dve.tensor_reduce(ms[:, b, 0, :], sq[:, :, 0:S_IN], AX_X, ALU.add)
                dve.tensor_reduce(ms[:, b, 1, :], sq[:, :, S_IN:F_IN], AX_X, ALU.add).then_inc(ms_ready, 1)

            def invert_rms(g):
                dve.wait_ge(rms_ready, 2 * g.done())
                dve.reciprocal(rms[:, g.parity], rms[:, g.parity]).then_inc(inverse_rms, 1)

            def scale_by_rms(g):
                b = g.parity
                dve.wait_ge(inverse_rms, g.done())
                dve.wait_ge(total_ready, g.done())
                for k, (a, c) in enumerate(((0, S_IN), (S_IN, F_IN))):
                    dve.tensor_tensor(y[:, b, :, a:c], y[:, b, :, a:c],
                                      rms[:, b, k, :].unsqueeze(2).broadcast_to([P, TILES, c - a]), ALU.mult) \
                        .then_inc(scaled, 1)

            def gate(g):
                b, n = g.parity, g.done(1)
                dve.wait_ge(total_ready, n)
                dve.wait_ge(sig_ready, n - GROUPS)
                if g.reuses:
                    dve.wait_ge(x1_ready, n - 2)
                dve.tensor_tensor(y[:, b, :, 0:S_IN], total[:, b, :, 0:S_IN], sig[:, :, 0:S_IN], ALU.mult)
                gates = sig[:, :, S_IN:OUT_S[1]].unsqueeze(2).broadcast_to([P, TILES, XYZ, V_IN])
                dve.tensor_tensor(y[:, b, :, S_IN:F_IN].rearrange("p j (c u) -> p j c u", c=XYZ),
                                  total[:, b, :, OUT_S[1]:ACC_W[1]].rearrange("p j (c u) -> p j c u", c=XYZ),
                                  gates, ALU.mult).then_inc(gated, 1)

            def add_and_moments(layer, g):
                b, n = g.parity, g.done(layer)
                dve.wait_ge(gated if layer else scaled, n - GROUPS if layer else 2 * n)
                dve.wait_ge(x_in[b], 16 * g.uses(layer))
                dve.tensor_tensor(y[:, b], y[:, b], xin[:, b], ALU.add).then_inc(y_sum, 1)
                dve.wait_ge(y_sum, n)
                for j in range(TILES):
                    last = dve.bn_stats(stats[:, j, :], y[:, b, j, :])
                last.then_inc(bn_done, 1)
                dve.wait_ge(bn_done, n)
                hold(dve)
                for j in range(TILES):
                    last = dve.bn_aggr(mv[:, b, j, :], stats[:, j, :])
                last.then_inc(var_ready, 1)

            def normalise(layer, g):
                b, n = g.parity, g.done(layer)
                dve.wait_ge(std_ready, n)
                dve.reciprocal(std[:, b], std[:, b]).then_inc(inverse_std, 1)
                dve.wait_ge(inverse_std, n)
                if layer or g.reuses:
                    dve.wait_ge(x1_out[b], 16 * (g.uses(layer) - 1))
                for j in range(TILES):
                    last = dve.tensor_scalar(x1[:, b, j, :], y[:, b, j, :], mv[:, b, j, 0:1], std[:, b, j:j + 1],
                                             ALU.subtract, ALU.mult)
                last.then_inc(x1_ready, 1)

            def features1(g):
                b = g.parity
                dve.wait_ge(node_mm, g.done(1))
                dve.wait_ge(sc_evac, g.done(1))
                dve.wait_ge(h_out[b], 16 * (g.uses(1) - 1))
                a = node_a[:, bass.ds(g.index * TILES, TILES)].unsqueeze(2)
                dve.tensor_tensor(h_sb[:, b, :, 0:P], node_psum4(2, 0, P),
                                  a.broadcast_to([P, TILES, P]), ALU.mult)
                dve.tensor_tensor(h_sb[:, b, :, P:F_IN], node_psum4(2, P + ACC_W[1], F_IN + ACC_W[1]),
                                  a.broadcast_to([P, TILES, V_IN]), ALU.mult).then_inc(h_evac, 1)

            walk(dve, (0, invert_rms), (1, sum_squares), (0, scale_by_rms), (-3, features1),
                 (0, lambda g: add_and_moments(0, g)), (-1, lambda g: normalise(0, g)))
            next_phase(dve, 3)
            edges(1)
            next_phase(dve, 4)
            walk(dve, (0, gate), (0, lambda g: add_and_moments(1, g)), (-1, lambda g: normalise(1, g)))
            next_phase(dve, 5)

        @block.tensor
        def _(pe):
            pe.wait_ge(weights_ready, len(scales))

            def project(layer, base, b, last_sem):
                os_ = OUT_S[layer]
                wa, wz = weight(f"node_a{layer}", 0, P), weight(f"node_b{layer}", 0, V_IN)
                z0 = P + os_ + 2 * V_IN
                for j in range(TILES):
                    pe.matmul(node_psum(base, j, 0, z0), xa[:, b, j * P:(j + 1) * P], wa, start=True, stop=True)
                    last = pe.matmul(node_psum(base, j, z0, z0 + 2 * V_IN), xz[:, b, j * P:(j + 1) * P], wz,
                                     start=True, stop=True)
                last.then_inc(last_sem, 1)

            def nodes_in(g):
                b = g.parity
                pe.wait_ge(xT_in[b], 32 * g.uses())
                if g.reuses:
                    pe.wait_ge(sc_evac, g.done() - 2)
                    pe.wait_ge(h_evac, g.done() - 2)
                project(0, TILES * b, b, node_mm)
            walk(pe, (0, nodes_in))
            next_phase(pe, 1)

            def edges(layer):
                os_, w = OUT_S[layer], ACC_W[layer]
                k1 = ATTR[layer]
                h0 = HID * (1 - layer)

                def hidden1(g):
                    b, n = g.parity, g.done(layer)
                    pe.wait_ge(attr_in[b], 32 * g.uses(layer))
                    hold(pe)
                    pe.matmul(H1_PS, weight(f"fc1_{layer}", 0, k1), attr[0:k1, b, :], start=True, stop=True) \
                        .then_inc(h1_mm, 1)

                def hidden2(g):
                    pe.wait_ge(h1_act, g.done(0))
                    hold(pe)
                    pe.matmul(H2_PS, weight("fc2_0", 0, HID), hidden[0:HID, :], start=True, stop=True).then_inc(h2_mm, 1)

                def edge_weights(g):
                    n = g.done(layer)
                    pe.wait_ge(h1_act if layer else h2_act, n)
                    for j in range(TILES):
                        last = pe.matmul(W_PS[:, j, 0:W_ALL], hidden[h0:h0 + HID, j * P:(j + 1) * P],
                                         weight(f"edge_w{layer}", h0, h0 + HID), start=True, stop=True)
                    last.then_inc(w_mm, 1)

                def turn(g, c):
                    n = g.done(layer)
                    c0, c1 = CHUNKS[c]
                    if c == 2:
                        pe.wait_ge(prod_ready, n)
                        pe.wait_ge(prodT_ready, 3 * (n - 1) + 1)
                    else:
                        pe.wait_ge(prod_part, 2 * (n - 1) + c + 1)
                    for j in range(TILES):
                        last = pe.transpose(T_PS[c % 2][0:c1 - c0, j * P:(j + 1) * P], prod[:, j, c0:c1], ident[:])
                    last.then_inc(prod_tr, 1)

                def project_messages(g):
                    n = g.done(layer)
                    pe.wait_ge(prodT_ready, 3 * n)
                    if not g.is_first:
                        pe.wait_ge(msg_ready, n - 1)
                        pe.wait_ge(s_ready, n - 1)
                    for j in range(TILES):
                        def pT(c, n_rows):
                            return prodT[0:n_rows, c, j * P:(j + 1) * P]
                        pe.matmul(O_PS[:, j, 0:V_IN + os_], pT(0, P), weight(f"outA{layer}", 0, P),
                                  start=True, stop=False, skip_group_check=True)
                        pe.matmul(O_PS[:, j, V_IN:V_IN + w], pT(1, P), weight(f"outB{layer}", 0, P),
                                  start=False, stop=False, skip_group_check=True)
                        last = pe.matmul(O_PS[:, j, V_IN + os_:V_IN + w], pT(2, V3), weight(f"outC{layer}", 0, V3),
                                         start=False, stop=True, skip_group_check=True)
                    last.then_inc(out_mm, 1)

                def merge(g):
                    b, n = g.parity, g.done(layer)
                    pe.wait_ge(same_ready, n)
                    pe.wait_ge(msg_ready, n)
                    pe.wait_ge(s_ready, n)
                    for q in range(2):
                        if q or not g.is_first:
                            pe.wait_ge(merged_half, 2 * (n - 1) + q)
                        for r in range(2):
                            j = 2 * q + r
                            last = pe.matmul(M_PS[:, r, 0:w], same[:, b, j, :], msg[:, j, 0:w], start=True, stop=True)
                        last.then_inc(merge_mm, 1)

                walk(pe, (1, hidden1), (0, lambda g: turn(g, 0)), (0, lambda g: turn(g, 1)), (0, lambda g: turn(g, 2)),
                     *[(1, hidden2)] * (1 - layer), (-1, merge), (1, edge_weights), (0, project_messages))

            edges(0)
            next_phase(pe, 2)

            def nodes_turn(g):
                b, n = g.parity, g.done(0)
                pe.wait_ge(x1_ready, n)
                hold(pe)
                for j in range(TILES):
                    pe.transpose(psum[:, j * P:(j + 1) * P], x1[:, b, j, 0:P], ident[:])
                    last = pe.transpose(psum[0:V_IN, BANK + j * P:BANK + (j + 1) * P], x1[:, b, j, P:F_IN], ident[:])
                last.then_inc(x1_tr, 1)
                pe.wait_ge(x1T_ready, 2 * n)
                if not g.is_first:
                    pe.wait_ge(sc_evac, g.done(1) - 1)
                    pe.wait_ge(h_evac, g.done(1) - 1)
                project(1, 2, 0, node_mm)
            walk(pe, (0, nodes_turn))
            next_phase(pe, 3)
            edges(1)
            next_phase(pe, 4)
            next_phase(pe, 5)


INS = ("x", "xT", "src_cols", "dst_cols", "src_rows", "dst_rows", "sh", "node_a", "attrT0", "attrT1", "gain",
       "sc_s0", "sc_v0", "lin_s0", "lin_v0", "fc1_0", "fc2_0", "fc_w0", "out_s0", "out_v0",
       "sc_s1", "sc_v1", "lin_s1", "lin_v1", "fc1_1", "fc_w1", "out_s1", "out_v1")


def kernel(x, src, dst, edge_attr_4, edge_attr_64, edge_attr_8, node_vec1, L0_gnn_W1_0, L0_gnn_W1_1, L0_gnn_Wfc1,
           L0_gnn_Wfc2, L0_gnn_Wfc3, L0_gnn_W2_0, L0_gnn_W2_1, L0_gnn_Wsc0, L0_gnn_Wsc1, L0_gnn_g0, L0_gnn_g1,
           L1_gnn_lin1_ws, L1_gnn_lin1_wv, L1_gnn_fc_w1, L1_gnn_fc_w2, L1_gnn_sc_ws, L1_gnn_sc_wv, L1_gnn_lin2_ws,
           L1_gnn_lin2_wv):
    import numpy as np
    import concourse.bacc as bacc
    from concourse.bass_utils import run_bass_kernel_spmd

    extra = N_PAD - N_NODES

    def padded(a, fill=0):
        return np.pad(np.asarray(a), ((0, extra),) + ((0, 0),) * (a.ndim - 1), constant_values=fill)

    def by_component(a):
        v = a[:, S_IN:].reshape(-1, V_IN, XYZ).transpose(0, 2, 1).reshape(-1, V3)
        return np.concatenate([a[:, :S_IN], v], 1)

    def columns(a):
        return a.reshape((COLS, P) + a.shape[1:]).swapaxes(0, 1).reshape(P, -1)

    xp = padded(by_component(np.asarray(x)))
    src_p, dst_p = padded(src, N_NODES), padded(dst, N_NODES)
    sh = padded(edge_attr_4)
    v = {
        "x": xp,
        "xT": xp.reshape(GROUPS, P, TILES, F_IN).transpose(0, 3, 2, 1).reshape(GROUPS, F_IN, ROWS),
        "src_cols": columns(src_p), "dst_cols": columns(dst_p),
        "src_rows": src_p.reshape(GROUPS, ROWS), "dst_rows": dst_p.reshape(GROUPS, ROWS),
        "sh": columns(np.concatenate([sh, sh[:, 1:2]], 1)),
        "node_a": padded(node_vec1).reshape(GROUPS, P, TILES).transpose(1, 0, 2).reshape(P, COLS),
        "attrT0": padded(edge_attr_8).reshape(GROUPS, ROWS, ATTR[0]).transpose(0, 2, 1),
        "attrT1": padded(edge_attr_64).reshape(GROUPS, ROWS, ATTR[1]).transpose(0, 2, 1),
        "gain": np.concatenate([np.asarray(L0_gnn_g0)] + [np.asarray(L0_gnn_g1)] * XYZ),
        "sc_s0": L0_gnn_Wsc0, "sc_v0": L0_gnn_Wsc1, "lin_s0": L0_gnn_W1_0, "lin_v0": L0_gnn_W1_1,
        "fc1_0": L0_gnn_Wfc1, "fc2_0": L0_gnn_Wfc2, "fc_w0": L0_gnn_Wfc3, "out_s0": L0_gnn_W2_0,
        "out_v0": L0_gnn_W2_1,
        "sc_s1": L1_gnn_sc_ws, "sc_v1": L1_gnn_sc_wv, "lin_s1": L1_gnn_lin1_ws, "lin_v1": L1_gnn_lin1_wv,
        "fc1_1": L1_gnn_fc_w1, "fc_w1": L1_gnn_fc_w2, "out_s1": L1_gnn_lin2_ws, "out_v1": L1_gnn_lin2_wv,
    }
    nc = bacc.Bacc("TRN2", target_bir_lowering=False, num_devices=1)
    arrays, aps = {}, {}
    for name in INS:
        a = np.ascontiguousarray(v[name])
        arrays["in_" + name] = a
        aps[name] = nc.dram_tensor("in_" + name, a.shape, mybir.dt.from_np(a.dtype), kind="ExternalInput").ap()
    out = nc.dram_tensor("out_nodes", (N_PAD, F_IN), F32, kind="ExternalOutput").ap()
    build(nc, aps, out)
    got = run_bass_kernel_spmd(nc, [arrays], core_ids=[0]).results[0]["out_nodes"][:N_NODES]
    vectors = got[:, S_IN:].reshape(-1, XYZ, V_IN).transpose(0, 2, 1).reshape(-1, V3)
    return np.concatenate([got[:, :S_IN], vectors], 1)
```

```python
from contextlib import ExitStack

import concourse.bass as bass
import concourse.mybir as mybir
from concourse.alu_op_type import AluOpType as ALU

ACT = mybir.ActivationFunctionType
F32 = mybir.dt.float32
I32 = mybir.dt.int32
AX_X = mybir.AxisListType.X

P = 128
TILES = 4
ROWS = P * TILES
HALF = ROWS // 2
N_NODES = 25000
GROUPS = -(-N_NODES // ROWS)
N_PAD = GROUPS * ROWS
COLS = GROUPS * TILES
TABLES = 2
S_IN, V_IN, XYZ = 64, 32, 3
V3 = V_IN * XYZ
F_IN = S_IN + V3
HID = 64
W_ALL = 2 * S_IN + 3 * V_IN
OUT_S = (64, 96)
Z_ROW = P - V_IN
ATTR = (8, 64)
SLOT = 256
BANK = 512
EPS = 1e-5
NEIGHBOURS = 16.0
HIDDEN_SCALE = (ATTR[0] ** -0.5, ATTR[1] ** -0.5)

def _columns(widths):
    at, out = 0, {}
    for name, n in widths:
        out[name] = (at, at + n)
        at += n
    return out, at


WEIGHT_COLS, WEIGHT_WIDTH = _columns([
    ("node_a0", 128 + 64 + 64), ("node_b0", 2 * V_IN), ("node_a1", 128 + 96 + 64), ("node_b1", 2 * V_IN),
    ("fc1_0", 2 * HID), ("fc2_0", 2 * HID), ("edge_w0", W_ALL), ("fc1_1", 2 * HID), ("edge_w1", W_ALL),
    ("outA0", V_IN + 64), ("outB0", 64 + V3), ("outC0", V3),
    ("outA1", V_IN + 96), ("outB1", 96 + V3), ("outC1", V3)])


class Group:

    def __init__(self, half, parity):
        self.half, self.parity = half, parity
        self.index = 2 * half + parity
        self.static = isinstance(half, int)
        self.reuses = not (self.static and half <= 0)
        self.is_first = self.static and self.index == 0
        self.is_last = self.static and self.index == GROUPS - 1

    def at(self, offset):
        halves, parity = divmod(self.parity + offset, 2)
        g = Group(self.half + halves, parity)
        return None if g.static and not 0 <= g.index < GROUPS else g

    def done(self, layer=0):
        return layer * GROUPS + self.index + 1

    def uses(self, layer=0):
        return layer * ((GROUPS + 1 - self.parity) // 2) + self.half + 1


def walk(eng, *stages):
    def step(g):
        for offset, stage in stages:
            if g.at(offset) is not None:
                stage(g.at(offset))
    for first in range(-max(offset for offset, _ in stages), 4):
        step(Group(first // 2, first % 2))
    with eng.Fori(2, GROUPS // 2) as i:
        step(Group(i, 0))
        step(Group(i, 1))
    for last in range(GROUPS - 1, GROUPS - min(0, min(offset for offset, _ in stages))):
        step(Group(last // 2, last % 2))


def build(nc, t, out):
    ctx = ExitStack()
    with ctx:
        def sb(name, shape, dt=F32):
            return ctx.enter_context(nc.sbuf_tensor(name, shape, dt))

        def ps(name, shape):
            return ctx.enter_context(nc.psum_tensor(name, shape, F32))

        def sem(name):
            return ctx.enter_context(nc.semaphore(name))

        def sem2(name):
            return [sem(f"{name}{b}") for b in range(2)]

        def dram(name, shape):
            return nc.dram_tensor(name, shape, F32).ap()

        h_tab = [dram("h_tab0", (N_PAD, F_IN)), dram("h_tab1", (N_PAD, F_IN))]
        ACC_W = [OUT_S[0] + V3, OUT_S[1] + V3]
        acc_tab = [[dram(f"acc_tab{l}{k}", (N_PAD + P, ACC_W[l])) for k in range(TABLES)] for l in range(2)]

        def rows(tab, g):
            r0 = g.index * ROWS
            return tab[bass.ds(r0, ROWS), :].rearrange("(p j) f -> p (j f)", j=TILES)

        W = sb("W", [P, WEIGHT_WIDTH])
        ident = sb("ident", [P, P])
        upto = sb("upto", [P, P])
        eps = sb("eps", [P, 1])
        minus_half = sb("minus_half", [P, TILES])
        gain = sb("gain", [P, F_IN])
        dump_row = sb("dump_row", [P, 1])
        zeros = sb("zeros", [P, ACC_W[1]])
        idx_i = [sb("src_i", [P, COLS], I32), sb("dst_i", [P, COLS], I32)]
        idx_f = [sb("src_f", [P, COLS]), sb("dst_f", [P, COLS])]
        repeats = sb("repeats", [P, 2, TILES])
        to_dump = sb("to_dump", [P, 2, COLS])
        from_row = sb("from_row", [P, 2, COLS])
        sh = sb("sh", [P, COLS, 5])
        node_a = sb("node_a", [P, COLS])
        x_all = sb("x_all", [P, COLS, F_IN])
        read_now = sb("read_now", [P, 2, TILES], I32)
        add_now = sb("add_now", [P, 2, TILES], I32)
        dump_part = sb("dump_part", [P, TILES])
        read_now_in, add_now_ready, dump_part_ready = sem2("read_now_in"), sem("add_now_ready"), sem("dump_part_ready")
        zero1_out = sem("zero1_out")

        def weight(name, p0, p1):
            c0, c1 = WEIGHT_COLS[name]
            return W[p0:p1, c0:c1]

        idx_row = sb("idx_row", [P, 2, ROWS], I32)
        AREA = 14080
        area = sb("area", [P, AREA])

        def carve(*shapes):
            at, views = 0, []
            for shape in shapes:
                n = 1
                for size in shape:
                    n *= size
                names = "abc"[:len(shape)]
                views.append(area[:, at:at + n].rearrange(f"p ({' '.join(names)}) -> p {' '.join(names)}",
                                                          **dict(zip(names, shape))))
                at += n
            assert at <= AREA, at
            return views

        xa, xz, sc_sb, h_sb, accs, y, total, sq, out_sb, sig = carve(
            (2, ROWS), (2, ROWS), (2, TILES, ACC_W[1]), (2, TILES, F_IN), (2, TABLES, TILES * ACC_W[1]),
            (2, TILES, F_IN), (2, TILES, ACC_W[1]), (TILES, F_IN), (2, TILES, F_IN), (2, TILES, OUT_S[1]))
        hg, attr, hidden1, hidden2, linear, crossed, other, prod, prodT, same, pw_sb, spread, msg, merged = carve(
            (2, TILES, F_IN), (2, HALF), (HALF,), (HALF,), (2, TILES, 224), (TILES, P), (TILES, V3),
            (TILES, 352), (3, ROWS), (2, TILES, P), (TILES, V_IN), (TILES, V3), (TILES, ACC_W[1]),
            (2, TILES, ACC_W[1]))
        ms = sb("ms", [P, 2, 2, TILES])
        rms = sb("rms", [P, 2, 2, TILES])
        stats = sb("stats", [P, TILES, 6])
        mv = sb("mv", [P, 2, TILES, 2])
        std = sb("std", [P, 2, TILES])
        shift = sb("shift", [P, 2, TILES])

        psum = ps("psum", [P, 8 * BANK])

        consts_ready, weights_in, weights_zero, weights_ready = (
            sem("consts_ready"), sem("weights_in"), sem("weights_zero"), sem("weights_ready"))
        xz_zero = sem("xz_zero")
        tables_in, more_weights_in = sem("tables_in"), sem("more_weights_in")
        idx_float, phase_end = sem("idx_float"), sem("phase_end")
        xT_in = sem2("xT_in")
        node_mm, sc_evac, h_evac = sem("node_mm"), sem("sc_evac"), sem("h_evac")
        shift_ready, x1_kept = sem("shift_ready"), sem("x1_kept")
        sc_out, h_out, zero_out = sem2("sc_out"), sem2("h_out"), sem("zero_out")
        to_dump_ready = sem("to_dump_ready")

        attr_zero, linear_ready = sem("attr_zero"), sem("linear_ready")
        attr_in, hg_in = sem2("attr_in"), sem2("hg_in")
        h1_mm, h1_act, h2_mm, h2_act, w_mm = (sem("h1_mm"), sem("h1_act"), sem("h2_mm"), sem("h2_act"), sem("w_mm"))
        u_dot, u_ready = sem("u_dot"), sem("u_ready")
        prod_ready, prod_tr, prodT_ready = sem("prod_ready"), sem("prod_tr"), sem("prodT_ready")
        out_mm, pw_ready, s_ready, spread_ready, msg_ready = (
            sem("out_mm"), sem("pw_ready"), sem("s_ready"), sem("spread_ready"), sem("msg_ready"))
        same_ready, merge_mm = sem("same_ready"), sem("merge_mm")
        added = [sem(f"added{k}") for k in range(TABLES)]

        acc_in, x_in, x1_out = sem2("acc_in"), sem("x_in"), sem2("x1_out")
        prod_part, merged_half = sem("prod_part"), sem("merged_half")
        gate_scaled = sem("gate_scaled")
        sq_ready, rms_ready, std_ready = sem("sq_ready"), sem("rms_ready"), sem("std_ready")
        var_eps = sem("var_eps")
        ms_ready, var_ready, x1_ready = sem("ms_ready"), sem("var_ready"), sem("x1_ready")
        x1_tr, x1T_ready = sem("x1_tr"), sem("x1T_ready")
        total_sum, total_ready, sig_ready, gated = sem("total_sum"), sem("total_ready"), sem("sig_ready"), sem("gated")
        y_sum, bn_done, inverse_rms, inverse_std = (
            sem("y_sum"), sem("bn_done"), sem("inverse_rms"), sem("inverse_std"))

        ENGINES = 5

        def next_phase(eng, k):
            eng.drain().then_inc(phase_end, 1)
            eng.wait_ge(phase_end, ENGINES * k)

        waits_held = sem("waits_held")

        def hold(eng):
            eng.sem_inc(waits_held, 1)

        def blocks(name, p0, c0, src):
            first = WEIGHT_COLS[name][0]
            return [(W[p0 + V_IN * c:p0 + V_IN * (c + 1), first + c0 + V_IN * c:first + c0 + V_IN * (c + 1)], src)
                    for c in range(XYZ)]

        def part(name, p0, p1, c0, c1, src):
            first = WEIGHT_COLS[name][0]
            return [(W[p0:p1, first + c0:first + c1], src)]

        weight_dmas = []
        for l in range(2):
            sc, scv, lin, linv = t[f"sc_s{l}"], t[f"sc_v{l}"], t[f"lin_s{l}"], t[f"lin_v{l}"]
            os_ = OUT_S[l]
            weight_dmas += part(f"node_a{l}", 0, S_IN, 0, S_IN, lin)
            weight_dmas += part(f"node_a{l}", 0, S_IN, P, P + os_, sc)
            for c in range(2):
                p0 = S_IN + V_IN * c
                weight_dmas += part(f"node_a{l}", p0, p0 + V_IN, p0, p0 + V_IN, linv)
                weight_dmas += part(f"node_a{l}", p0, p0 + V_IN, P + os_ + V_IN * c, P + os_ + V_IN * (c + 1), scv)
            z0 = Z_ROW
            weight_dmas += part(f"node_b{l}", z0, z0 + V_IN, 0, V_IN, scv)
            weight_dmas += part(f"node_b{l}", z0, z0 + V_IN, V_IN, 2 * V_IN, linv)
            if l == 0:
                first_weight_dmas, weight_dmas = weight_dmas, []
            fc = t[f"fc_w{l}"]
            for q in range(2):
                for c0, c1, f0 in ((0, 64, 64), (64, 128, 0), (128, W_ALL, 128)):
                    weight_dmas += part(f"edge_w{l}", HID * q, HID * (q + 1), c0, c1, fc[:, f0:f0 + c1 - c0])
                weight_dmas += part(f"fc1_{l}", ATTR[l] * q, ATTR[l] * (q + 1), HID * q, HID * (q + 1), t[f"fc1_{l}"])
            o_s, o_v = t[f"out_s{l}"], t[f"out_v{l}"]
            weight_dmas += part(f"outA{l}", 0, 64, 0, V_IN, o_v[0:64, :])
            weight_dmas += part(f"outA{l}", 64, 128, V_IN, V_IN + os_, o_s[0:64, :])
            weight_dmas += part(f"outB{l}", V3, P, 0, os_, o_s[64:96, :])
            weight_dmas += blocks(f"outB{l}", 0, os_, o_v[64:96, :]) + blocks(f"outC{l}", 0, 0, o_v[96:128, :])
        for q in range(2):
            weight_dmas += part("fc2_0", HID * q, HID * (q + 1), HID * q, HID * (q + 1), t["fc2_0"])

        scales = []
        for l in range(2):
            def cols(name, a, b):
                c = WEIGHT_COLS[name][0]
                return (c + a, c + b)
            os_ = OUT_S[l]
            f_s = (96 * NEIGHBOURS) ** -0.5
            f_v = (128 * NEIGHBOURS) ** -0.5
            node_scales = [(cols(f"node_a{l}", 0, S_IN), S_IN ** -0.5), (cols(f"node_a{l}", S_IN, P), V_IN ** -0.5),
                       (cols(f"node_a{l}", P, P + os_), S_IN ** -0.5),
                       (cols(f"node_a{l}", P + os_, P + os_ + 2 * V_IN), V_IN ** -0.5),
                       (cols(f"node_b{l}", 0, 2 * V_IN), V_IN ** -0.5)]
            if l == 0:
                first_scales, node_scales = node_scales, []
            scales += node_scales
            scales += [(cols(f"edge_w{l}", 0, 160), HID ** -0.5),
                       (cols(f"edge_w{l}", 160, 192), (HID * 3) ** -0.5),
                       (cols(f"edge_w{l}", 192, 224), (HID * 2) ** -0.5),
                       (cols(f"outA{l}", 0, V_IN), f_v), (cols(f"outA{l}", V_IN, V_IN + os_), f_s),
                       (cols(f"outB{l}", 0, os_), f_s), (cols(f"outB{l}", os_, os_ + V3), f_v),
                       (cols(f"outC{l}", 0, V3), f_v)]

        def node_psum(base, j, a, b):
            return psum[:, (base + j) * BANK + a:(base + j) * BANK + b]

        def node_psum4(base, a, b):
            return psum[:, base * BANK:(base + TILES) * BANK].rearrange("p (j c) -> p j c", j=TILES)[:, :, a:b]

        def turned_psum(parity, part):
            bank = 6 * parity + part
            return psum[:, bank * BANK:(bank + 1) * BANK]

        def pair_psum(q, a, b):
            return psum[:, (2 + 2 * q) * BANK:(4 + 2 * q) * BANK].rearrange("p (j c) -> p j c", j=2)[:, :, a:b]

        def sc_flat(g, layer):
            return sc_sb[:, g.parity].rearrange("p j f -> p (j f)")[:, 0:TILES * ACC_W[layer]]

        def x_of(g):
            return x_all[:, bass.ds(g.index * TILES, TILES), :]

        def x_tile(g, j, a, b):
            return x_all[:, bass.ds(g.index * TILES + j, 1), a:b].rearrange("p t f -> p (t f)")

        def zero_rows(w):
            return zeros[:, 0:w].unsqueeze(1).broadcast_to([P, TILES, w])

        H1_PS = psum[:, 0:HALF]
        H2_PS = psum[:, HALF:BANK]
        W_PS = psum[:, BANK:3 * BANK].rearrange("p (j c) -> p j c", c=SLOT)
        T_PS = [psum[:, 3 * BANK:4 * BANK], psum[:, 4 * BANK:5 * BANK]]
        O_PS = psum[:, 5 * BANK:7 * BANK].rearrange("p (j c) -> p j c", c=SLOT)
        M_PS = psum[:, 7 * BANK:8 * BANK].rearrange("p (j c) -> p j c", c=SLOT)
        CHUNKS = ((0, 128), (128, 256), (256, 352))

        block = ctx.enter_context(nc.Block())

        @block.sync
        def _(sp):
            sp.wait_ge(weights_zero, 1)
            for dst, src in first_weight_dmas:
                sp.dma_start(dst, src).then_inc(weights_in, 16)
            for k in range(2):
                sp.dma_start(idx_i[k][:], t[("src", "dst")[k] + "_cols"][:]).then_inc(tables_in, 16)
            sp.dma_start(sh[:], t["sh"].rearrange("p (c k) -> p c k", k=5)).then_inc(tables_in, 16)
            sp.dma_start(node_a[:], t["node_a"]).then_inc(tables_in, 16)
            sp.dma_start(gain[:], t["gain"].partition_broadcast(P)).then_inc(tables_in, 16)

            def load_nodes(g):
                b = g.parity
                if g.reuses:
                    sp.wait_ge(node_mm, g.done() - 2)
                sp.dma_start(xa[:, b, :], t["xT"][g.index, 0:P, :]).then_inc(xT_in[b], 16)
                sp.dma_start(xz[Z_ROW:P, b, :], t["xT"][g.index, P:F_IN, :]).then_inc(xT_in[b], 16)
            walk(sp, (0, load_nodes))
            next_phase(sp, 1)

            def load_edges(layer):
                k_add, k_read = ("src", "dst")[layer] + "_rows", ("dst", "src")[layer] + "_cols"

                def step(g):
                    b = g.parity
                    if g.reuses:
                        sp.wait_ge(hg_in[b], 16 * TILES * (g.uses(layer) - 1))
                    sp.dma_start(read_now[:, b, :], t[k_read][:, bass.ds(g.index * TILES, TILES)]) \
                        .then_inc(read_now_in[b], 16)
                    if g.reuses:
                        sp.wait_ge(h1_mm, g.done(layer) - 2)
                        sp.wait_ge(same_ready, g.done(layer) - 2)
                    sp.dma_start(attr[0:2 * ATTR[layer], b, :], t[f"attrT{layer}"][g.index]).then_inc(attr_in[b], 16)
                    sp.dma_start(idx_row[:, b, :], t[k_add][g.index, :].partition_broadcast(P)).then_inc(attr_in[b], 16)
                    if layer == 0:
                        sp.dma_start(rows(acc_tab[1][1], g).rearrange("p (j f) -> p j f", j=TILES),
                                     zero_rows(ACC_W[1])).then_inc(zero1_out, 16)
                        sp.dma_start(x_of(g).rearrange("p j f -> p (j f)"), rows(t["x"], g)).then_inc(x_in, 16)
                walk(sp, (0, step))

            def load_sums(layer):
                w = ACC_W[layer]

                def step(g):
                    b = g.parity
                    if g.reuses:
                        sp.wait_ge(total_sum, g.done(layer) - 2)
                    for k in range(TABLES):
                        sp.dma_start(accs[:, b, k, 0:TILES * w], rows(acc_tab[layer][k], g)).then_inc(acc_in[b], 16)
                walk(sp, (0, step))

            sp.wait_ge(attr_zero, 1)
            load_edges(0)
            sp.wait_ge(zero1_out, 16 * GROUPS)
            sp.wait_ge(x_in, 16 * GROUPS)
            next_phase(sp, 2)
            load_sums(0)
            next_phase(sp, 3)
            load_edges(1)
            next_phase(sp, 4)
            load_sums(1)
            next_phase(sp, 5)

        @block.gpsimd
        def _(pool):
            pool.memset(W[:], 0.0).then_inc(weights_zero, 1)
            pool.memset(xz[0:Z_ROW], 0.0).then_inc(xz_zero, 1)
            pool.memset(ident[:], 0.0).then_inc(consts_ready, 1)
            pool.memset(upto[:], 1.0).then_inc(consts_ready, 1)
            pool.memset(zeros[:], 0.0).then_inc(consts_ready, 1)
            pool.memset(eps[:], EPS).then_inc(consts_ready, 1)
            pool.memset(minus_half[:], -0.5).then_inc(consts_ready, 1)
            pool.iota(dump_row[:], pattern=[[0, 1]], base=N_PAD, channel_multiplier=1,
                      allow_small_or_imprecise_dtypes=True).then_inc(consts_ready, 1)
            pool.wait_ge(consts_ready, 6)
            pool.affine_select(out=ident[:], in_=ident[:], compare_op=ALU.not_equal, fill=1.0, base=0,
                               pattern=[[-1, P]], channel_multiplier=1).then_inc(consts_ready, 1)
            pool.affine_select(out=upto[:], in_=upto[:], compare_op=ALU.is_ge, fill=0.0, base=0,
                               pattern=[[-1, P]], channel_multiplier=1).then_inc(consts_ready, 1)

            with pool.Fori(0, GROUPS) as i:
                pool.dma_start(acc_tab[0][1][bass.ds(i * ROWS, ROWS), :].rearrange("(p j) f -> p j f", j=TILES),
                               zero_rows(ACC_W[0])).then_inc(zero_out, 16)
            for dst, src in weight_dmas:
                pool.dma_start(dst, src).then_inc(more_weights_in, 16)
            for l in range(2):
                for k in range(TABLES):
                    pool.dma_start(acc_tab[l][k][N_PAD:N_PAD + P, :], zeros[:, 0:ACC_W[l]]).then_inc(zero_out, 16)
            pool.wait_ge(zero_out, 16 * (2 * TABLES + GROUPS))
            next_phase(pool, 1)

            def edges(layer):
                w = ACC_W[layer]

                def gather(g, j):
                    b = g.parity
                    if j == 0:
                        if g.reuses:
                            pool.wait_ge(linear_ready, g.done(layer) - 2)
                            pool.wait_ge(u_ready, g.done(layer) - 2)
                        pool.wait_ge(read_now_in[b], 16 * g.uses(layer))
                        hold(pool)
                    pool.indirect_dma_start(
                        out=hg[:, b, j, :], out_offset=None, in_=h_tab[layer][:, :],
                        in_offset=bass.IndirectOffsetOnAxis(ap=read_now[:, b, j:j + 1], axis=0)).then_inc(hg_in[b], 16)

                def scatter(g, j):
                    b, k = g.parity, j % TABLES
                    pool.wait_ge(add_now_ready, g.done(layer))
                    pool.wait_ge(merged_half, 2 * (g.done(layer) - 1) + j // 2 + 1)
                    before_this = layer * COLS // TABLES + g.index * (TILES // TABLES) + j // TABLES
                    if not g.static or before_this:
                        pool.wait_ge(added[k], 16 * before_this)
                    hold(pool)
                    pool.indirect_dma_start(
                        out=acc_tab[layer][k][:, :],
                        out_offset=bass.IndirectOffsetOnAxis(ap=add_now[:, b, j:j + 1], axis=0),
                        in_=merged[:, b, j, 0:w], in_offset=None, compute_op=ALU.add).then_inc(added[k], 16)

                walk(pool, (1, lambda g: gather(g, 0)), (1, lambda g: gather(g, 1)),
                     (-3, lambda g: scatter(g, 0)), (-3, lambda g: scatter(g, 1)),
                     (1, lambda g: gather(g, 2)), (1, lambda g: gather(g, 3)),
                     (-3, lambda g: scatter(g, 2)), (-3, lambda g: scatter(g, 3)))
                for k in range(TABLES):
                    pool.wait_ge(added[k], 16 * (layer + 1) * COLS // TABLES)

            def totals(layer):
                w = ACC_W[layer]

                def flat(g):
                    return total[:, g.parity].rearrange("p j f -> p (j f)")[:, 0:TILES * w]

                def add_tables(g):
                    b, n = g.parity, g.done(layer)
                    pool.wait_ge(acc_in[b], 16 * TABLES * g.uses(layer))
                    if g.reuses:
                        if layer == 0:
                            pool.wait_ge(sq_ready, n - 2)
                            pool.wait_ge(total_ready, n - 2)
                        else:
                            pool.wait_ge(gated, g.done() - 2)
                    pool.tensor_tensor(flat(g), accs[:, b, 0, 0:TILES * w], accs[:, b, 1, 0:TILES * w], ALU.add) \
                        .then_inc(total_sum, 1)

                def gained(g):
                    b, n = g.parity, g.done(layer)
                    pool.wait_ge(total_sum, n)
                    if g.reuses:
                        pool.wait_ge(y_sum, n - 2)
                    pool.tensor_tensor(y[:, b], flat(g).rearrange("p (j f) -> p j f", j=TILES),
                                       gain[:].unsqueeze(1).broadcast_to([P, TILES, w]), ALU.mult) \
                        .then_inc(total_ready, 1)

                def inverse_deviation(g):
                    b = g.parity
                    pool.wait_ge(var_ready, g.done(1))
                    if g.reuses:
                        pool.wait_ge(x1_ready, g.done(1) - 2)
                    hold(pool)
                    pool.tensor_scalar(std[:, b], mv[:, b, :, 1], EPS, None, ALU.add).then_inc(var_eps, 1)
                    pool.wait_ge(var_eps, g.done())
                    pool.tensor_tensor(std[:, b], std[:, b], minus_half[:], ALU.pow).then_inc(inverse_std, 1)
                walk(pool, (1, add_tables), (0, gained) if layer == 0 else (-1, inverse_deviation))

            pool.memset(attr, 0.0).then_inc(attr_zero, 1)
            edges(0)
            next_phase(pool, 2)
            totals(0)
            next_phase(pool, 3)
            edges(1)
            next_phase(pool, 4)
            totals(1)
            next_phase(pool, 5)

        @block.scalar
        def _(act):

            def self_out(g):
                b, w = g.parity, ACC_W[0]
                act.wait_ge(node_mm, g.done())
                if g.reuses:
                    act.wait_ge(sc_out[b], 16 * (g.uses() - 1))
                act.activation(sc_flat(g, 0).rearrange("p (j f) -> p j f", j=TILES), node_psum4(TILES * b, P, P + w),
                               ACT.Copy).then_inc(sc_evac, 1)

            def store_self(layer, g):
                act.wait_ge(sc_evac, g.done(layer))
                act.dma_start(rows(acc_tab[layer][0], g), sc_flat(g, layer)).then_inc(sc_out[g.parity], 16)

            def features_out(layer, g):
                b = g.parity
                act.wait_ge(h_evac, g.done(layer))
                act.dma_start(rows(h_tab[layer], g), h_sb[:, b].rearrange("p j f -> p (j f)")).then_inc(h_out[b], 16)

            def stores_landed(layer):
                for b in range(2):
                    last = (layer + 1) * ((GROUPS + 1 - b) // 2)
                    act.wait_ge(sc_out[b], 16 * last)
                    act.wait_ge(h_out[b], 16 * last)

            walk(act, (0, self_out), (0, lambda g: store_self(0, g)), (-1, lambda g: features_out(0, g)))
            stores_landed(0)
            next_phase(act, 1)

            def edges(layer):
                os_, w = OUT_S[layer], ACC_W[layer]

                def first_silu(g):
                    n = g.done(layer)
                    act.wait_ge(h1_mm, n)
                    act.activation(hidden1, H1_PS, ACT.Silu, scale=HIDDEN_SCALE[layer]).then_inc(h1_act, 1)

                def second_silu(g):
                    act.wait_ge(h2_mm, g.done(0))
                    act.activation(hidden2, H2_PS, ACT.Silu, scale=HID ** -0.5).then_inc(h2_act, 1)

                def turned_out(g, c):
                    n3 = 3 * (g.done(layer) - 1) + c + 1
                    n_rows = CHUNKS[c][1] - CHUNKS[c][0]
                    act.wait_ge(prod_tr, n3)
                    act.activation(prodT[0:n_rows, c, :], T_PS[c % 2][0:n_rows, :], ACT.Copy).then_inc(prodT_ready, 1)

                def merged_out(g):
                    b = g.parity
                    if g.reuses:
                        for k in range(TABLES):
                            base = layer * COLS // TABLES
                            act.wait_ge(added[k], 16 * (base + (g.index - 1) * (TILES // TABLES)))
                    for q in range(2):
                        act.wait_ge(merge_mm, 2 * (g.done(layer) - 1) + q + 1)
                        act.activation(merged[:, b, 2 * q:2 * q + 2, 0:w], M_PS[:, :, 0:w], ACT.Copy) \
                            .then_inc(merged_half, 1)

                def linear_parts(g):
                    b, n = g.parity, g.done(layer)
                    act.wait_ge(hg_in[b], 16 * TILES * g.uses(layer))
                    if g.reuses:
                        act.wait_ge(prod_ready, n - 2)
                    act.activation(linear[:, b, :, 0:S_IN], hg[:, b, :, 0:S_IN], ACT.Copy)
                    for j in range(TILES):
                        sh0 = sh[:, bass.ds(g.index * TILES + j, 1), 0:1].rearrange("p t k -> p (t k)")
                        last = act.activation(linear[:, b, j, S_IN:224], hg[:, b, j, :], ACT.Copy, scale=sh0)
                    last.then_inc(linear_ready, 1)

                def message_out(g):
                    n = g.done(layer)
                    act.wait_ge(out_mm, n)
                    if not g.is_first:
                        act.wait_ge(spread_ready, n - 1)
                    act.activation(pw_sb[:], O_PS[:, :, 0:V_IN], ACT.Copy).then_inc(pw_ready, 1)
                    if not g.is_first:
                        act.wait_ge(merge_mm, 2 * (n - 1))
                    act.activation(msg[:, :, 0:os_], O_PS[:, :, V_IN:V_IN + os_], ACT.Copy).then_inc(s_ready, 1)

                walk(act, (1, first_silu), (0, lambda g: turned_out(g, 0)), (0, lambda g: turned_out(g, 1)),
                     (0, lambda g: turned_out(g, 2)), *[(1, second_silu)] * (1 - layer), (-1, merged_out),
                     (1, linear_parts), (0, message_out))

            edges(0)
            next_phase(act, 2)

            def squares(g):
                act.wait_ge(total_sum, g.done())
                if not g.is_first:
                    act.wait_ge(ms_ready, g.done() - 1)
                act.activation(sq.rearrange("p j f -> p (j f)"),
                               total[:, g.parity].rearrange("p j f -> p (j f)")[:, 0:TILES * F_IN],
                               ACT.Square).then_inc(sq_ready, 1)

            def root_mean_squares(g):
                b = g.parity
                act.wait_ge(ms_ready, g.done())
                for k, n_channels in enumerate((S_IN, V_IN)):
                    act.activation(rms[:, b, k, :], ms[:, b, k, :], ACT.Sqrt, bias=eps[:, 0:1],
                                   scale=1.0 / n_channels).then_inc(rms_ready, 1)

            def deviation(g):
                act.wait_ge(var_ready, g.done())
                if g.reuses:
                    act.wait_ge(x1_ready, g.done() - 2)
                act.activation(std[:, g.parity], mv[:, g.parity, :, 1], ACT.Sqrt, bias=eps[:, 0:1], scale=1.0) \
                    .then_inc(std_ready, 1)

            def normalise(layer, g):
                b, n = g.parity, g.done(layer)
                act.wait_ge(shift_ready, n)
                if layer and g.reuses:
                    act.wait_ge(x1_out[b], 16 * (g.uses() - 1))
                for j in range(TILES):
                    last = act.activation(out_sb[:, b, j, :], (y if layer else out_sb)[:, b, j, :],
                                          ACT.Identity, bias=shift[:, b, j:j + 1], scale=std[:, b, j:j + 1])
                last.then_inc(x1_ready, 1)

            def turned_nodes(g):
                act.wait_ge(x1_tr, g.done())
                if g.reuses:
                    act.wait_ge(node_mm, 2 * (g.done() - 2) + GROUPS)
                act.activation(xa[:, g.parity, :], turned_psum(g.parity, 0), ACT.Copy).then_inc(x1T_ready, 1)
                act.activation(xz[:, g.parity, :], turned_psum(g.parity, 1), ACT.Copy).then_inc(x1T_ready, 1)

            def self1(g):
                b = g.parity
                act.wait_ge(sc_out[b], 16 * (g.uses(1) - 1))
                for q in range(2):
                    act.wait_ge(node_mm, GROUPS + 2 * g.index + q + 1)
                    act.activation(sc_sb[:, b, 2 * q:2 * q + 2, :], pair_psum(q, P, P + ACC_W[1]), ACT.Copy) \
                        .then_inc(sc_evac, 1)

            def store_self1(g):
                act.wait_ge(sc_evac, GROUPS + 2 * g.done())
                act.dma_start(rows(acc_tab[1][0], g), sc_flat(g, 1)).then_inc(sc_out[g.parity], 16)

            def store_features1(g):
                b = g.parity
                act.wait_ge(h_evac, GROUPS + 2 * g.done())
                act.dma_start(rows(h_tab[1], g), h_sb[:, b].rearrange("p j f -> p (j f)")).then_inc(h_out[b], 16)

            walk(act, (-1, deviation), (-4, self1), (-4, store_self1), (1, squares), (-2, turned_nodes),
                 (-1, lambda g: normalise(0, g)), (1, root_mean_squares), (-4, store_features1))
            stores_landed(1)
            next_phase(act, 3)
            edges(1)
            next_phase(act, 4)

            def gates(g):
                act.wait_ge(total_sum, g.done(1))
                if g.reuses:
                    act.wait_ge(gated, g.done() - 2)
                for j in range(TILES):
                    last = act.activation(sig[:, g.parity, j, :], total[:, g.parity, j, 0:OUT_S[1]], ACT.Sigmoid,
                                          scale=node_a[:, bass.ds(g.index * TILES + j, 1)])
                last.then_inc(sig_ready, 1)

            def store_nodes(g):
                act.wait_ge(x1_ready, g.done(1))
                act.dma_start(rows(out, g), out_sb[:, g.parity].rearrange("p j f -> p (j f)")) \
                    .then_inc(x1_out[g.parity], 16)
            walk(act, (1, gates), (-1, lambda g: normalise(1, g)),
                 (-1, store_nodes))
            for b in range(2):
                act.wait_ge(x1_out[b], 16 * ((GROUPS + 1 - b) // 2))
            next_phase(act, 5)

        @block.vector
        def _(dve):
            dve.wait_ge(weights_in, 16 * len(first_weight_dmas))
            for (c0, c1), f in first_scales:
                dve.tensor_scalar(W[:, c0:c1], W[:, c0:c1], f, None, ALU.mult).then_inc(weights_ready, 1)
            dve.wait_ge(tables_in, 16 * 5)
            dve.wait_ge(consts_ready, 8)
            for k in range(2):
                dve.tensor_copy(idx_f[k][:], idx_i[k][:]).then_inc(idx_float, 1)
            dve.wait_ge(idx_float, 2)

            def node_features(g):
                b = g.parity
                dve.wait_ge(node_mm, g.done())
                if g.reuses:
                    dve.wait_ge(h_out[b], 16 * (g.uses() - 1))
                dve.wait_ge(sc_evac, g.done())
                dve.tensor_copy(h_sb[:, b, :, 0:P], node_psum4(TILES * b, 0, P))
                dve.tensor_copy(h_sb[:, b, :, P:F_IN], node_psum4(TILES * b, P + ACC_W[0], F_IN + ACC_W[0])) \
                    .then_inc(h_evac, 1)
            walk(dve, (0, node_features))
            for k in range(2):
                dve.tensor_scalar(to_dump[:, k], idx_f[k][:], -1.0, dump_row[:, 0:1], ALU.mult, ALU.add) \
                    .then_inc(to_dump_ready, 1)
            dve.wait_ge(to_dump_ready, 2)
            for k in range(2):
                dve.tensor_tensor(from_row[:, k], idx_f[k][:], to_dump[:, k], ALU.subtract)
            dve.wait_ge(more_weights_in, 16 * len(weight_dmas))
            for (c0, c1), f in scales:
                dve.tensor_scalar(W[:, c0:c1], W[:, c0:c1], f, None, ALU.mult).then_inc(weights_ready, 1)
            next_phase(dve, 1)

            def edges(layer):
                os_, w = OUT_S[layer], ACC_W[layer]

                def edge_sh(g, k, n, width):
                    v = sh[:, bass.ds(g.index * TILES, TILES), k:k + n]
                    return v.unsqueeze(3).broadcast_to([P, TILES, n, width])

                def directions(g):
                    b, n = g.parity, g.done(layer)
                    v = hg[:, b, :, S_IN:F_IN].rearrange("p j (c u) -> p j c u", c=XYZ)
                    cross = crossed[:, :, V_IN:P].rearrange("p j (c u) -> p j c u", c=XYZ)
                    rest = other.rearrange("p j (c u) -> p j c u", c=XYZ)
                    dot = crossed[:, :, 0:V_IN]
                    dve.wait_ge(hg_in[b], 16 * TILES * g.uses(layer))
                    if not g.is_first:
                        dve.wait_ge(prod_ready, n - 1)
                    dve.tensor_tensor(cross[:, :, 0:2], v[:, :, 1:3], edge_sh(g, 3, 2, V_IN), ALU.mult)
                    dve.tensor_tensor(cross[:, :, 2:3], v[:, :, 0:1], edge_sh(g, 2, 1, V_IN), ALU.mult)
                    dve.tensor_tensor(rest[:, :, 1:3], v[:, :, 0:2], edge_sh(g, 3, 2, V_IN), ALU.mult)
                    dve.tensor_tensor(rest[:, :, 0:1], v[:, :, 2:3], edge_sh(g, 2, 1, V_IN), ALU.mult) \
                        .then_inc(u_dot, 1)
                    dve.wait_ge(u_dot, 4 * (n - 1) + 1)
                    dve.tensor_tensor(cross, cross, rest, ALU.subtract).then_inc(u_dot, 1)
                    dve.wait_ge(u_dot, 4 * (n - 1) + 2)
                    dve.tensor_tensor(rest, v, edge_sh(g, 1, 3, V_IN), ALU.mult).then_inc(u_dot, 1)
                    dve.wait_ge(u_dot, 4 * (n - 1) + 3)
                    dve.tensor_tensor(dot, rest[:, :, 0], rest[:, :, 1], ALU.add).then_inc(u_dot, 1)
                    dve.wait_ge(u_dot, 4 * n)
                    dve.tensor_tensor(dot, dot, rest[:, :, 2], ALU.add).then_inc(u_ready, 1)

                def same_rows(g):
                    b, n = g.parity, g.done(layer)
                    dve.wait_ge(attr_in[b], 32 * g.uses(layer))
                    if g.reuses:
                        dve.wait_ge(merge_mm, 2 * (n - 2))
                    idx_q = idx_row[:, b, :].rearrange("p (j q) -> p j q", j=TILES)
                    for j in range(TILES):
                        last = dve.scalar_tensor_tensor(
                            out=same[:, b, j, :], in0=idx_q[:, j, :],
                            scalar=idx_f[layer][:, bass.ds(g.index * TILES + j, 1)], in1=upto[:], op0=ALU.is_equal,
                            op1=ALU.mult, accum_out=repeats[:, b, j:j + 1])
                    last.then_inc(same_ready, 1)

                def rows_to_add(g):
                    b, n = g.parity, g.done(layer)
                    dve.wait_ge(same_ready, n)
                    cols = bass.ds(g.index * TILES, TILES)
                    dve.scalar_tensor_tensor(out=dump_part[:], in0=repeats[:, b, :], scalar=2.0,
                                             in1=to_dump[:, layer, cols], op0=ALU.min, op1=ALU.mult) \
                        .then_inc(dump_part_ready, 1)
                    dve.wait_ge(dump_part_ready, n)
                    if g.reuses:
                        base = layer * COLS // TABLES
                        for k in range(TABLES):
                            dve.wait_ge(added[k], 16 * (base + (g.index - 1) * (TILES // TABLES)))
                    dve.tensor_tensor(add_now[:, b, :], dump_part[:], from_row[:, layer, cols], ALU.add) \
                        .then_inc(add_now_ready, 1)

                def products(g):
                    b, n = g.parity, g.done(layer)
                    dve.wait_ge(w_mm, n)
                    dve.wait_ge(u_ready, n)
                    dve.wait_ge(linear_ready, n)
                    dve.tensor_tensor(prod[:, :, 0:128], W_PS[:, :, 0:128], linear[:, b, :, 0:128], ALU.mult) \
                        .then_inc(prod_part, 1)

                    def spread_w(c0):
                        return W_PS[:, :, c0:c0 + V_IN].unsqueeze(2).broadcast_to([P, TILES, XYZ, V_IN])

                    def xyz(ap):
                        return ap.rearrange("p j (c u) -> p j c u", c=XYZ)
                    dve.tensor_tensor(xyz(prod[:, :, 128:224]), spread_w(128), xyz(linear[:, b, :, 128:224]), ALU.mult)
                    dve.tensor_tensor(prod[:, :, 224:256], W_PS[:, :, 160:192], crossed[:, :, 0:V_IN], ALU.mult) \
                        .then_inc(prod_part, 1)
                    dve.tensor_tensor(xyz(prod[:, :, 256:352]), spread_w(192), xyz(crossed[:, :, V_IN:P]), ALU.mult) \
                        .then_inc(prod_ready, 1)

                def messages(g):
                    n = g.done(layer)
                    dve.wait_ge(pw_ready, n)
                    pw = pw_sb[:].unsqueeze(2).broadcast_to([P, TILES, XYZ, V_IN])
                    dve.tensor_tensor(spread[:].rearrange("p j (c u) -> p j c u", c=XYZ), pw,
                                      edge_sh(g, 1, 3, V_IN), ALU.mult).then_inc(spread_ready, 1)
                    dve.wait_ge(spread_ready, n)
                    dve.wait_ge(s_ready, n)
                    if not g.is_first:
                        dve.wait_ge(merge_mm, 2 * (n - 1))
                    dve.tensor_tensor(msg[:, :, os_:w], O_PS[:, :, V_IN + os_:V_IN + w], spread[:], ALU.add) \
                        .then_inc(msg_ready, 1)

                walk(dve, (0, products), (-1, messages), (-1, rows_to_add), (1, directions), (1, same_rows))

            edges(0)
            next_phase(dve, 2)

            def sum_squares(g):
                b = g.parity
                dve.wait_ge(sq_ready, g.done())
                dve.tensor_reduce(ms[:, b, 0, :], sq[:, :, 0:S_IN], AX_X, ALU.add)
                dve.tensor_reduce(ms[:, b, 1, :], sq[:, :, S_IN:F_IN], AX_X, ALU.add).then_inc(ms_ready, 1)

            def invert_rms(g):
                dve.wait_ge(rms_ready, 2 * g.done())
                dve.reciprocal(rms[:, g.parity], rms[:, g.parity]).then_inc(inverse_rms, 1)

            def scale_and_add(g):
                b = g.parity
                if g.reuses:
                    dve.wait_ge(x1_tr, g.done() - 2)
                    dve.wait_ge(x1_kept, g.done() - 2)
                dve.wait_ge(inverse_rms, g.done())
                dve.wait_ge(total_ready, g.done())
                for j in range(TILES):
                    for k, (a, c) in enumerate(((0, S_IN), (S_IN, F_IN))):
                        last = dve.scalar_tensor_tensor(
                            out=out_sb[:, b, j, a:c], in0=y[:, b, j, a:c], scalar=rms[:, b, k, j:j + 1],
                            in1=x_tile(g, j, a, c), op0=ALU.mult, op1=ALU.add)
                last.then_inc(y_sum, 1)

            def gate(g):
                b, n = g.parity, g.done()
                dve.wait_ge(total_sum, g.done(1))
                dve.wait_ge(gate_scaled, n)
                if g.reuses:
                    dve.wait_ge(x1_ready, g.done(1) - 2)
                dve.tensor_tensor(y[:, b, :, 0:S_IN], total[:, b, :, 0:S_IN], sig[:, b, :, 0:S_IN], ALU.mult)
                gates = sig[:, b, :, S_IN:OUT_S[1]].unsqueeze(2).broadcast_to([P, TILES, XYZ, V_IN])
                dve.tensor_tensor(y[:, b, :, S_IN:F_IN].rearrange("p j (c u) -> p j c u", c=XYZ),
                                  total[:, b, :, OUT_S[1]:ACC_W[1]].rearrange("p j (c u) -> p j c u", c=XYZ),
                                  gates, ALU.mult).then_inc(gated, 1)

            def scale_gates(g):
                dve.wait_ge(sig_ready, g.done())
                a = node_a[:, bass.ds(g.index * TILES, TILES)].unsqueeze(2).broadcast_to([P, TILES, OUT_S[1]])
                dve.tensor_tensor(sig[:, g.parity], sig[:, g.parity], a, ALU.mult).then_inc(gate_scaled, 1)

            def add_x(g):
                b = g.parity
                dve.wait_ge(gated, g.done())
                dve.tensor_tensor(y[:, b], y[:, b], x_of(g), ALU.add).then_inc(y_sum, 1)

            def moments(layer, g):
                dve.wait_ge(y_sum, g.done(layer))
                for j in range(TILES):
                    last = dve.bn_stats(stats[:, j, :], (y if layer else out_sb)[:, g.parity, j, :])
                last.then_inc(bn_done, 1)

            def mean_and_variance(layer, g):
                dve.wait_ge(bn_done, g.done(layer))
                hold(dve)
                for j in range(TILES):
                    last = dve.bn_aggr(mv[:, g.parity, j, :], stats[:, j, :])
                last.then_inc(var_ready, 1)

            def invert_deviation(g):
                dve.wait_ge(std_ready, g.done())
                dve.reciprocal(std[:, g.parity], std[:, g.parity]).then_inc(inverse_std, 1)

            def shifts(layer, g):
                b, n = g.parity, g.done(layer)
                dve.wait_ge(inverse_std, n)
                if g.reuses:
                    dve.wait_ge(x1_ready, n - 2)
                dve.scalar_tensor_tensor(out=shift[:, b], in0=mv[:, b, :, 0], scalar=-1.0, in1=std[:, b],
                                         op0=ALU.mult, op1=ALU.mult).then_inc(shift_ready, 1)

            def features1(g):
                b = g.parity
                dve.wait_ge(h_out[b], 16 * (g.uses(1) - 1))
                for q in range(2):
                    dve.wait_ge(sc_evac, GROUPS + 2 * g.index + q + 1)
                    a = node_a[:, bass.ds(g.index * TILES + 2 * q, 2)].unsqueeze(2)
                    h = h_sb[:, b, 2 * q:2 * q + 2, :]
                    dve.tensor_tensor(h[:, :, 0:P], pair_psum(q, 0, P), a.broadcast_to([P, 2, P]), ALU.mult)
                    dve.tensor_tensor(h[:, :, P:F_IN], pair_psum(q, P + ACC_W[1], F_IN + ACC_W[1]),
                                      a.broadcast_to([P, 2, V_IN]), ALU.mult).then_inc(h_evac, 1)

            def keep(g):
                dve.wait_ge(x1_ready, g.done())
                dve.tensor_copy(x_of(g), out_sb[:, g.parity]).then_inc(x1_kept, 1)

            walk(dve, (-1, invert_deviation), (-2, keep), (-1, lambda g: shifts(0, g)), (0, invert_rms),
                 (-4, features1), (0, scale_and_add), (0, lambda g: moments(0, g)), (1, sum_squares),
                 (0, lambda g: mean_and_variance(0, g)))
            next_phase(dve, 3)
            edges(1)
            next_phase(dve, 4)
            walk(dve, (0, gate), (0, add_x), (-1, lambda g: shifts(1, g)), (0, lambda g: moments(1, g)),
                 (1, scale_gates), (0, lambda g: mean_and_variance(1, g)))
            next_phase(dve, 5)

        @block.tensor
        def _(pe):
            pe.wait_ge(weights_ready, len(first_scales))
            pe.wait_ge(xz_zero, 1)

            def project(layer, base, b, last_sem, tiles=range(TILES)):
                os_ = OUT_S[layer]
                wa, wz = weight(f"node_a{layer}", 0, P), weight(f"node_b{layer}", 0, P)
                z0 = P + os_ + 2 * V_IN
                for j in tiles:
                    pe.matmul(node_psum(base, j, 0, z0), xa[:, b, j * P:(j + 1) * P], wa, start=True, stop=True)
                    last = pe.matmul(node_psum(base, j, z0, z0 + 2 * V_IN), xz[:, b, j * P:(j + 1) * P], wz,
                                     start=True, stop=True)
                last.then_inc(last_sem, 1)

            def nodes_in(g):
                b = g.parity
                pe.wait_ge(xT_in[b], 32 * g.uses())
                if g.reuses:
                    pe.wait_ge(sc_evac, g.done() - 2)
                    pe.wait_ge(h_evac, g.done() - 2)
                project(0, TILES * b, b, node_mm)
            walk(pe, (0, nodes_in))
            next_phase(pe, 1)
            pe.wait_ge(weights_ready, len(first_scales) + len(scales))

            def edges(layer):
                os_, w = OUT_S[layer], ACC_W[layer]
                last_hidden = hidden1 if layer else hidden2

                def first_hidden(g):
                    b, n = g.parity, g.done(layer)
                    pe.wait_ge(attr_in[b], 32 * g.uses(layer))
                    hold(pe)
                    pe.matmul(H1_PS, weight(f"fc1_{layer}", 0, P), attr[:, b, :], start=True, stop=True) \
                        .then_inc(h1_mm, 1)

                def second_hidden(g):
                    pe.wait_ge(h1_act, g.done(0))
                    hold(pe)
                    pe.matmul(H2_PS, weight("fc2_0", 0, P), hidden1, start=True, stop=True).then_inc(h2_mm, 1)

                def edge_weights(g):
                    n = g.done(layer)
                    pe.wait_ge(h1_act if layer else h2_act, n)
                    for j in range(TILES):
                        h0, c0 = HID * (j // 2), P * (j % 2)
                        last = pe.matmul(W_PS[:, j, 0:W_ALL], last_hidden[h0:h0 + HID, c0:c0 + P],
                                         weight(f"edge_w{layer}", h0, h0 + HID), start=True, stop=True)
                    last.then_inc(w_mm, 1)

                def turn(g, c):
                    n = g.done(layer)
                    c0, c1 = CHUNKS[c]
                    if c == 2:
                        pe.wait_ge(prod_ready, n)
                        pe.wait_ge(prodT_ready, 3 * (n - 1) + 1)
                    else:
                        pe.wait_ge(prod_part, 2 * (n - 1) + c + 1)
                    for j in range(TILES):
                        last = pe.transpose(T_PS[c % 2][0:c1 - c0, j * P:(j + 1) * P], prod[:, j, c0:c1], ident[:])
                    last.then_inc(prod_tr, 1)

                def project_messages(g):
                    n = g.done(layer)
                    pe.wait_ge(prodT_ready, 3 * n)
                    if not g.is_first:
                        pe.wait_ge(msg_ready, n - 1)
                        pe.wait_ge(s_ready, n - 1)
                    for j in range(TILES):
                        def pT(c, n_rows):
                            return prodT[0:n_rows, c, j * P:(j + 1) * P]
                        pe.matmul(O_PS[:, j, 0:V_IN + os_], pT(0, P), weight(f"outA{layer}", 0, P),
                                  start=True, stop=False, skip_group_check=True)
                        pe.matmul(O_PS[:, j, V_IN:V_IN + w], pT(1, P), weight(f"outB{layer}", 0, P),
                                  start=False, stop=False, skip_group_check=True)
                        last = pe.matmul(O_PS[:, j, V_IN + os_:V_IN + w], pT(2, V3), weight(f"outC{layer}", 0, V3),
                                         start=False, stop=True, skip_group_check=True)
                    last.then_inc(out_mm, 1)

                def merge(g):
                    b, n = g.parity, g.done(layer)
                    pe.wait_ge(same_ready, n)
                    pe.wait_ge(msg_ready, n)
                    pe.wait_ge(s_ready, n)
                    for q in range(2):
                        if q or not g.is_first:
                            pe.wait_ge(merged_half, 2 * (n - 1) + q)
                        for r in range(2):
                            j = 2 * q + r
                            last = pe.matmul(M_PS[:, r, 0:w], same[:, b, j, :], msg[:, j, 0:w], start=True, stop=True)
                        last.then_inc(merge_mm, 1)

                walk(pe, (1, first_hidden), *[(0, lambda g, c=c: turn(g, c)) for c in range(len(CHUNKS))],
                     *[(1, second_hidden)] * (1 - layer), (-1, merge), (1, edge_weights), (0, project_messages))

            edges(0)
            next_phase(pe, 2)

            def nodes_turn(g):
                b = g.parity
                if g.reuses:
                    pe.wait_ge(x1T_ready, 2 * (g.done() - 2))
                pe.wait_ge(x1_ready, g.done())
                hold(pe)
                for j in range(TILES):
                    pe.transpose(turned_psum(b, 0)[:, j * P:(j + 1) * P], out_sb[:, b, j, 0:P], ident[:])
                    last = pe.transpose(turned_psum(b, 1)[:, j * P:(j + 1) * P], out_sb[:, b, j, V_IN:F_IN], ident[:])
                last.then_inc(x1_tr, 1)

            def nodes_project(g):
                pe.wait_ge(x1T_ready, 2 * g.done())
                for q in range(2):
                    if not g.is_first:
                        pe.wait_ge(h_evac, GROUPS + 2 * (g.index - 1) + q + 1)
                    project(1, 2, g.parity, node_mm, range(2 * q, 2 * q + 2))
            walk(pe, (0, nodes_turn), (-1, nodes_project))
            next_phase(pe, 3)
            edges(1)
            next_phase(pe, 4)
            next_phase(pe, 5)


INS = ("x", "xT", "src_cols", "dst_cols", "src_rows", "dst_rows", "sh", "node_a", "attrT0", "attrT1", "gain",
       "sc_s0", "sc_v0", "lin_s0", "lin_v0", "fc1_0", "fc2_0", "fc_w0", "out_s0", "out_v0",
       "sc_s1", "sc_v1", "lin_s1", "lin_v1", "fc1_1", "fc_w1", "out_s1", "out_v1")


def kernel(x, src, dst, edge_attr_4, edge_attr_64, edge_attr_8, node_vec1, L0_gnn_W1_0, L0_gnn_W1_1, L0_gnn_Wfc1,
           L0_gnn_Wfc2, L0_gnn_Wfc3, L0_gnn_W2_0, L0_gnn_W2_1, L0_gnn_Wsc0, L0_gnn_Wsc1, L0_gnn_g0, L0_gnn_g1,
           L1_gnn_lin1_ws, L1_gnn_lin1_wv, L1_gnn_fc_w1, L1_gnn_fc_w2, L1_gnn_sc_ws, L1_gnn_sc_wv, L1_gnn_lin2_ws,
           L1_gnn_lin2_wv):
    import numpy as np
    import concourse.bacc as bacc
    from concourse.bass_utils import run_bass_kernel_spmd

    extra = N_PAD - N_NODES

    def padded(a, fill=0):
        return np.pad(np.asarray(a), ((0, extra),) + ((0, 0),) * (a.ndim - 1), constant_values=fill)

    def by_component(a):
        v = a[:, S_IN:].reshape(-1, V_IN, XYZ).transpose(0, 2, 1).reshape(-1, V3)
        return np.concatenate([a[:, :S_IN], v], 1)

    def columns(a):
        return a.reshape((COLS, P) + a.shape[1:]).swapaxes(0, 1).reshape(P, -1)

    def halves(a):
        return padded(a).reshape(GROUPS, 2, HALF, -1).transpose(0, 1, 3, 2).reshape(GROUPS, -1, HALF)

    xp = padded(by_component(np.asarray(x)))
    src_p, dst_p = padded(src, N_NODES), padded(dst, N_NODES)
    sh = padded(edge_attr_4)
    v = {
        "x": xp,
        "xT": xp.reshape(GROUPS, P, TILES, F_IN).transpose(0, 3, 2, 1).reshape(GROUPS, F_IN, ROWS),
        "src_cols": columns(src_p), "dst_cols": columns(dst_p),
        "src_rows": src_p.reshape(GROUPS, ROWS), "dst_rows": dst_p.reshape(GROUPS, ROWS),
        "sh": columns(np.concatenate([sh, sh[:, 1:2]], 1)),
        "node_a": padded(node_vec1).reshape(GROUPS, P, TILES).transpose(1, 0, 2).reshape(P, COLS),
        "attrT0": halves(edge_attr_8), "attrT1": halves(edge_attr_64),
        "gain": np.concatenate([np.asarray(L0_gnn_g0)] + [np.asarray(L0_gnn_g1)] * XYZ),
        "sc_s0": L0_gnn_Wsc0, "sc_v0": L0_gnn_Wsc1, "lin_s0": L0_gnn_W1_0, "lin_v0": L0_gnn_W1_1,
        "fc1_0": L0_gnn_Wfc1, "fc2_0": L0_gnn_Wfc2, "fc_w0": L0_gnn_Wfc3, "out_s0": L0_gnn_W2_0,
        "out_v0": L0_gnn_W2_1,
        "sc_s1": L1_gnn_sc_ws, "sc_v1": L1_gnn_sc_wv, "lin_s1": L1_gnn_lin1_ws, "lin_v1": L1_gnn_lin1_wv,
        "fc1_1": L1_gnn_fc_w1, "fc_w1": L1_gnn_fc_w2, "out_s1": L1_gnn_lin2_ws, "out_v1": L1_gnn_lin2_wv,
    }
    nc = bacc.Bacc("TRN2", target_bir_lowering=False, num_devices=1)
    arrays, aps = {}, {}
    for name in INS:
        a = np.ascontiguousarray(v[name])
        arrays["in_" + name] = a
        aps[name] = nc.dram_tensor("in_" + name, a.shape, mybir.dt.from_np(a.dtype), kind="ExternalInput").ap()
    out = nc.dram_tensor("out_nodes", (N_PAD, F_IN), F32, kind="ExternalOutput").ap()
    build(nc, aps, out)
    got = run_bass_kernel_spmd(nc, [arrays], core_ids=[0]).results[0]["out_nodes"][:N_NODES]
    vectors = got[:, S_IN:].reshape(-1, XYZ, V_IN).transpose(0, 2, 1).reshape(-1, V3)
    return np.concatenate([got[:, :S_IN], vectors], 1)
```
